# Optimizing a Trainium2 kernel written in Bass

```python
import numpy as np
import jax
import jax.numpy as jnp

def _softmax(x, axis=-1):
    return jax.nn.softmax(x, axis=axis)

def _gelu(x):
    return jax.nn.gelu(x, approximate=True)

def _silu(x):
    return jax.nn.silu(x)

def _sigmoid(x):
    return jax.nn.sigmoid(x)

def _layernorm(x, axis=-1, eps=1e-05):
    m = jnp.mean(x, axis=axis, keepdims=True)
    v = jnp.var(x, axis=axis, keepdims=True)
    return (x - m) / jnp.sqrt(v + eps)

def _scatter_add(tgt, idx, src, axis=0):
    return tgt.at[idx].add(src)

def _segment_sum(src, seg, n):
    return jax.ops.segment_sum(src, seg, n)
kernel_name = 'mk_flamingo_gated_d1_seqx_r8_a9c8e6'

def setup_inputs(seed: int=0):
    np.random.seed(seed)
    _w = jnp.asarray

    def _rec_inputs():
        import jax
        import jax.numpy as jnp
        _rk = jax.random.key(seed)
        x = -0.0003929 + 0.9999 * jax.random.normal(jax.random.fold_in(_rk, 1), (16, 128, 256), jnp.float32)
        _lenS = 128 - jax.random.randint(jax.random.fold_in(_rk, 7), (16,), 0, max(1, 128 // 4) + 1, jnp.int32)
        _lenS2 = 128 - jax.random.randint(jax.random.fold_in(_rk, 8), (16,), 0, max(1, 128 // 4) + 1, jnp.int32)
        _ctx_2048P = jax.random.normal(jax.random.fold_in(_rk, 11), (16, 16, 256), jnp.float32)
        _ctx_2048c = jax.random.dirichlet(jax.random.fold_in(_rk, 511), 0.3 * jnp.ones((16,), jnp.float32), (16, 128))
        _ctx_2048t = jnp.einsum('bsk,bkd->bsd', _ctx_2048c, _ctx_2048P)
        _ctx_2048t = _ctx_2048t * jax.lax.rsqrt(jnp.mean(jnp.square(_ctx_2048t)) + 1e-12) * 0.953939
        ctx_2048 = -0.000514642 + 1.00011 * (_ctx_2048t + 0.3 * jax.random.normal(jax.random.fold_in(_rk, 611), (16, 128, 256), jnp.float32))
        _g = jax.random.normal(jax.random.fold_in(_rk, 9001), (2, 1), jnp.float32)
        _g = jnp.sign(_g) * jnp.maximum(jnp.abs(_g), 1.0) + (_g == 0) * 1.0
        g_xattn = _g[0]
        g_ffn = _g[1]
        return (x, ctx_2048, g_xattn, g_ffn)
    x, ctx_2048, g_xattn, g_ffn = _rec_inputs()

    def _L0_xattn_setup():
        import jax, jax.numpy as jnp
        import numpy as np
        DIM = 256
        NHEADS = 32
        HEAD_DIM = DIM // NHEADS
        EPS = 1e-06

        def _rmsnorm(t):
            return t * jax.lax.rsqrt(jnp.mean(t * t, axis=-1, keepdims=True) + EPS)
        key = jax.random.key(seed)
        kx, kc, kq, kk, kv = jax.random.split(key, 5)
        x = jax.random.normal(kx, (2, 512, DIM), dtype=jnp.float32)
        context = jax.random.normal(kc, (2, 64, DIM), dtype=jnp.float32)
        std = 0.02
        Wq = jax.random.normal(kq, (DIM, DIM), dtype=jnp.float32) * std
        Wk = jax.random.normal(kk, (DIM, DIM), dtype=jnp.float32) * std
        Wv = jax.random.normal(kv, (DIM, DIM), dtype=jnp.float32) * std
        return {'x': x, 'context': context, 'Wq': Wq, 'Wk': Wk, 'Wv': Wv}
    _L0_xattn_all = _L0_xattn_setup()
    _L0_xattn_in = {k: v for k, v in _L0_xattn_all.items() if k in ('Wq', 'Wk', 'Wv')}
    del _L0_xattn_all

    def _L0_ffn_setup():
        import jax, jax.numpy as jnp
        import numpy as np
        DIM = 256
        HID = 704
        ZERO_POINT = 128.0

        def _qlinear(x, wq, scale):
            W = (wq.astype(jnp.float32) - ZERO_POINT) * scale[:, None]
            return jnp.einsum('bsd,hd->bsh', x, W)
        key = jax.random.key(seed)
        ks = jax.random.split(key, 7)
        B, S = (4, 256)
        sg = jax.random.uniform(ks[1], (HID,)) * (0.02 / np.sqrt(DIM)) + 0.0001
        su = jax.random.uniform(ks[3], (HID,)) * (0.02 / np.sqrt(DIM)) + 0.0001
        sd = jax.random.uniform(ks[5], (DIM,)) * (0.02 / np.sqrt(HID)) + 0.0001
        return {'x': jax.random.normal(ks[0], (B, S, DIM), dtype=jnp.float32), 'wq_gate': jax.random.randint(ks[2], (HID, DIM), 0, 32, dtype=jnp.int32), 's_gate': sg, 'wq_up': jax.random.randint(ks[4], (HID, DIM), 0, 32, dtype=jnp.int32), 's_up': su, 'wq_down': jax.random.randint(ks[6], (DIM, HID), 0, 32, dtype=jnp.int32), 's_down': sd}
    _L0_ffn_all = _L0_ffn_setup()
    _L0_ffn_in = {k: v for k, v in _L0_ffn_all.items() if k in ('wq_gate', 's_gate', 'wq_up', 's_up', 'wq_down', 's_down')}
    del _L0_ffn_all
    return {'x': x, 'ctx_2048': ctx_2048, 'g_xattn': g_xattn, 'g_ffn': g_ffn, 'L0_xattn_Wq': _L0_xattn_in['Wq'], 'L0_xattn_Wk': _L0_xattn_in['Wk'], 'L0_xattn_Wv': _L0_xattn_in['Wv'], 'L0_ffn_wq_gate': _L0_ffn_in['wq_gate'], 'L0_ffn_s_gate': _L0_ffn_in['s_gate'], 'L0_ffn_wq_up': _L0_ffn_in['wq_up'], 'L0_ffn_s_up': _L0_ffn_in['s_up'], 'L0_ffn_wq_down': _L0_ffn_in['wq_down'], 'L0_ffn_s_down': _L0_ffn_in['s_down']}

def reference(x, ctx_2048, g_xattn, g_ffn, L0_xattn_Wq, L0_xattn_Wk, L0_xattn_Wv, L0_ffn_wq_gate, L0_ffn_s_gate, L0_ffn_wq_up, L0_ffn_s_up, L0_ffn_wq_down, L0_ffn_s_down):
    import jax
    import jax.numpy as jnp

    def _L0_xattn_ref(x, context, Wq, Wk, Wv):
        import jax, jax.numpy as jnp
        import numpy as np
        DIM = 256
        NHEADS = 32
        HEAD_DIM = DIM // NHEADS
        EPS = 1e-06

        def _rmsnorm(t):
            return t * jax.lax.rsqrt(jnp.mean(t * t, axis=-1, keepdims=True) + EPS)
        b, n, _ = x.shape
        m = context.shape[1]
        q = x @ Wq.T
        k_raw = context @ Wk.T
        v_raw = context @ Wv.T
        q = q.reshape(b, n, NHEADS, HEAD_DIM).transpose(0, 2, 1, 3)
        kv = jnp.concatenate([k_raw, v_raw], axis=-1)
        kv = kv.reshape(b, m, NHEADS, HEAD_DIM, 2)
        k = kv[..., 0].transpose(0, 2, 1, 3)
        v = kv[..., 1].transpose(0, 2, 1, 3)
        q = _rmsnorm(q)
        k = _rmsnorm(k)
        scale = HEAD_DIM ** (-0.5)
        scores = jnp.einsum('bhnd,bhmd->bhnm', q, k) * scale
        attn = jax.nn.softmax(scores, axis=-1)
        out = jnp.einsum('bhnm,bhmd->bhnd', attn, v)
        return out.transpose(0, 2, 1, 3).reshape(b, n, NHEADS * HEAD_DIM)

    def _L0_ffn_ref(x, wq_gate, s_gate, wq_up, s_up, wq_down, s_down):
        import jax, jax.numpy as jnp
        import numpy as np
        DIM = 256
        HID = 704
        ZERO_POINT = 128.0

        def _qlinear(x, wq, scale):
            W = (wq.astype(jnp.float32) - ZERO_POINT) * scale[:, None]
            return jnp.einsum('bsd,hd->bsh', x, W)
        gate = _qlinear(x, wq_gate, s_gate)
        gate = jax.nn.silu(gate)
        up = _qlinear(x, wq_up, s_up)
        return _qlinear(gate * up, wq_down, s_down)
    x = x + jnp.tanh(g_xattn[0]) * _L0_xattn_ref(_layernorm(x, axis=-1), ctx_2048, L0_xattn_Wq, L0_xattn_Wk, L0_xattn_Wv)
    x = x + jnp.tanh(g_ffn[0]) * _L0_ffn_ref(_layernorm(x, axis=-1), L0_ffn_wq_gate, L0_ffn_s_gate, L0_ffn_wq_up, L0_ffn_s_up, L0_ffn_wq_down, L0_ffn_s_down)
    return x

_drawn_inputs = setup_inputs


def setup_inputs(seed=0):
    import zlib

    import numpy as np

    out = dict(_drawn_inputs(seed))
    spreads = {}
    factors = {'L0_ffn_s_gate': 8.0, 'L0_ffn_s_up': 8.0, 'L0_ffn_s_down': 8.0}
    for name, (base, spread) in spreads.items():
        noise = np.random.default_rng([zlib.crc32(name.encode()), seed]).standard_normal(out[name].shape)
        drawn = base * np.exp(spread * noise) if base else spread * noise
        out[name] = jnp.asarray(drawn.astype(out[name].dtype))
    for name, factor in factors.items():
        out[name] = (out[name] * factor).astype(out[name].dtype)
    return out
```

```python
from contextlib import ExitStack

import concourse.bass as bass
from concourse import mybir

ALU = mybir.AluOpType
ACT = mybir.ActivationFunctionType
AX = mybir.AxisListType
F32 = mybir.dt.float32
F32R = mybir.dt.float32r
F16 = mybir.dt.float16
I32 = mybir.dt.int32

P = 128
HD = 8
LN_EPS = 1e-5
RMS_EPS = 1e-6
ZERO_POINT = 128.0

MID_SCALE = 0.375 ** 0.2
START_SCALE = (0.375 * MID_SCALE) ** 0.2
START_BITS = 1594644007.0
RSQRT_STEPS = 9
BLOCK = 32
SLOTW = HD + 1
HEADS_PER_OCTET = 8
LOOP = False


def build_program(nc, x, ctx, g_xattn, g_ffn, Wq, Wk, Wv, wq_gate, s_gate, wq_up, s_up, wq_down, s_down, out):
    B, S, D = x.shape
    HID = wq_gate.shape[0]
    H = D // HD
    KC = D // P
    NJ = -(-HID // P)
    LAST = HID - (NJ - 1) * P
    PAIRS = B // 2
    OCTETS = H // HEADS_PER_OCTET
    GROUPS = H // 4
    TOK = 2 * S
    assert S == P and D == 2 * P and H == 32 and B % 2 == 0 and NJ == 6

    def rows(j):
        return P if j < NJ - 1 else LAST

    def place(n):
        region, i, quadrant = (n // 12, n % 12 // 4, n % 4) if n < 24 else (2, (n - 24) // 4, n % 4)
        head = 12 * region + 3 * quadrant + i if region < 2 else 24 + 2 * quadrant + i
        return head, region, quadrant, i

    TASKS = ["turn0", "ffn3", "ffn4", "out0", "stackq0", "stackk0", "qk0", "v0", "ffn5", "y0",
             "turn1", "turn2", "y1", "out1", "stackq1", "stackk1", "qk1", "v1", "ffn0", "ffn1", "ffn2"]
    PREP = {"ffn3": 0, "ffn4": 1, "ffn5": 2, "y0": 3, "turn2": 4, "y1": 5, "ffn0": 6, "ffn1": 7, "ffn2": 8}
    NBANK = 3

    def exists(p, task):
        if task in PREP and p == 0:
            return True
        if task in ("ffn3", "ffn4", "ffn5", "y0", "y1"):
            return 0 <= p - 2 < PAIRS
        if task in ("turn2", "ffn0", "ffn1", "ffn2"):
            return 0 <= p - 1 < PAIRS
        b = 2 * p + int(task[-1])
        ahead = {"out": -1, "sta": 1, "v": 1, "v0": 1, "v1": 1, "tur": 2, "qk0": 2, "qk1": 2}[task[:3]]
        return 0 <= b + ahead < B

    FIRST, FIRST_STEADY, LAST_STEADY = -2, 2, PAIRS - 2

    def use(p, task):
        pos = TASKS.index(task)
        q = p if isinstance(p, int) else FIRST_STEADY
        n = sum(exists(i, t) for i in range(FIRST, q + 1) for k, t in enumerate(TASKS)
                if k % NBANK == pos % NBANK and (i < q or k <= pos))
        return pos % NBANK, n if isinstance(p, int) else n + len(TASKS) // NBANK * (p - FIRST_STEADY)

    def since(v, least):
        return v >= least if isinstance(v, int) else True

    with ExitStack() as stack:
        def sb(name, shape, dt=F32):
            return stack.enter_context(nc.sbuf_tensor(name, shape, dt))

        def sem(name):
            return stack.enter_context(nc.semaphore(name))

        x_all = sb("x_all", [P, B, D])
        ctx_sb = sb("ctx_sb", [P, 2, D])
        w_raw = sb("w_raw", [P, 3, KC, D])
        w_hi = sb("w_hi", [P, KC, 3 * D], F32R)
        w_lo = sb("w_lo", [P, KC, 3 * D], F32R)
        gu_int = sb("gu_int", [P, 2, NJ, D], I32)
        dn_int = sb("dn_int", [P, KC, HID], I32)
        gu_raw = sb("gu_raw", [P, 2, NJ, D])
        dn_raw = sb("dn_raw", [P, KC, HID])
        gu_hi = sb("gu_hi", [P, NJ, 2, KC, P], F32R)
        gu_lo = sb("gu_lo", [P, NJ, 2, KC, P], F32R)
        dn_hi = sb("dn_hi", [P, NJ, D], F32R)
        dn_lo = sb("dn_lo", [P, NJ, D], F32R)
        scales = sb("scales", [P, 3, NJ])
        half_gate = sb("half_gate", [P, NJ])
        down_scale = sb("down_scale", [P, D])
        gates = sb("gates", [P, 2])
        tanh_gates = sb("tanh_gates", [P, 2])
        ident = sb("ident", [P, P])
        ident16 = sb("ident16", [P, P], F16)
        stats = sb("stats", [P, 2, 6])
        mean_var = sb("mean_var", [P, 2, 2])
        xn = sb("xn", [P, 2, D])
        x1n = sb("x1n", [P, 2, D])
        root_in = sb("root_in", [P, 2 * H + 2])
        root_y = sb("root_y", [P, 2 * H + 2])
        root_xy = sb("root_xy", [P, 2 * H + 2])
        root_v = sb("root_v", [P, 2 * H + 2])
        root_p = sb("root_p", [P, 2 * H + 2])
        xc_hi = sb("xc_hi", [P, 2, 2 * KC, P], F32R)
        xc_lo = sb("xc_lo", [P, 2, 2 * KC, P], F32R)
        squares = sb("squares", [P, 2 * D])
        sums = sb("sums", [P, 2 * H])
        qk_unit = sb("qk_unit", [P, 2 * H, HD])
        qk_parts = sb("qk_parts", [P, 2 * H, 4, HD], F16)
        q_stack = sb("q_stack", [P, 2, GROUPS, P], F16)
        k_stack = sb("k_stack", [P, 2, GROUPS, P], F16)
        k_masked = sb("k_masked", [P, 2, 4, GROUPS, P], F16)
        v_blocks = sb("v_blocks", [P, 2, H * BLOCK])
        probs = sb("probs", [P, 2, HEADS_PER_OCTET * P])
        o_turned = sb("o_turned", [P, 2, 3 * P])
        inv_den = sb("inv_den", [P, 12, 3])
        attn = sb("attn", [P, D])
        x2_hi = sb("x2_hi", [P, KC, TOK], F32R)
        x2_lo = sb("x2_lo", [P, KC, TOK], F32R)
        tanh_g = sb("tanh_g", [P, 2, TOK])
        silu2 = sb("silu2", [P, 2, TOK])
        hidden = sb("hidden", [P, 2, TOK])
        h_hi = sb("h_hi", [P, NJ, TOK], F32R)
        h_lo = sb("h_lo", [P, NJ, TOK], F32R)
        y_scaled = sb("y_scaled", [P, 2, D])

        score_ps = [stack.enter_context(nc.psum_tensor(f"score_ps{i}", [P, HEADS_PER_OCTET, P], F32)) for i in range(2)]
        pv_ps = stack.enter_context(nc.psum_tensor("pv_ps", [P, 512], F32))
        bank = [stack.enter_context(nc.psum_tensor(f"bank{i}", [P, 512], F32)) for i in range(NBANK)]

        w_loaded = sem("w_loaded")
        x_loaded = [sem(f"x_loaded{i}") for i in range(3)]
        ctx_loaded = [sem(f"ctx_loaded{i}") for i in range(2)]
        ffn_w_loaded = sem("ffn_w_loaded")
        small_loaded = sem("small_loaded")
        km_loaded = [sem(f"km_loaded{i}") for i in range(2)]
        stored = sem("stored")
        ident_zeroed = sem("ident_zeroed")
        ident_ready = sem("ident_ready")
        ident16_ready = sem("ident16_ready")
        km_zeroed = sem("km_zeroed")
        v_zeroed = sem("v_zeroed")
        v_ready_ones = sem("v_ready_ones")
        consts_ready = sem("consts_ready")
        tanh_ready = sem("tanh_ready")
        scale_steps = sem("scale_steps")
        w_converted = sem("w_converted")
        w_turned = sem("w_turned")
        w_hi_ready = sem("w_hi_ready")
        w_lo_ready = sem("w_lo_ready")
        prep_hi = sem("prep_hi")
        prep_lo = sem("prep_lo")
        filled = [sem(f"filled{i}") for i in range(NBANK)]
        drained = [sem(f"drained{i}") for i in range(NBANK)]
        ctx_turned = sem("ctx_turned")
        stats_ready = sem("stats_ready")
        mean_ready = sem("mean_ready")
        xn_ready = sem("xn_ready")
        stats2_ready = sem("stats2_ready")
        mean2_ready = sem("mean2_ready")
        x1n_ready = sem("x1n_ready")
        root_in_ready = sem("root_in_ready")
        root_steps = sem("root_steps")
        xc_hi_ready = sem("xc_hi_ready")
        xc_lo_ready = sem("xc_lo_ready")
        squares_ready = sem("squares_ready")
        sums_ready = sem("sums_ready")
        qk_hi_ready = sem("qk_hi_ready")
        qk_lo_ready = sem("qk_lo_ready")
        qk_parts_ready = sem("qk_parts_ready")
        scores_ready = sem("scores_ready")
        probs_ready = sem("probs_ready")
        pv_done = sem("pv_done")
        o_turned_ready = sem("o_turned_ready")
        inv_den_ready = sem("inv_den_ready")
        attn_ready = sem("attn_ready")
        x1_ready = sem("x1_ready")
        x2_hi_ready = sem("x2_hi_ready")
        x2_lo_ready = sem("x2_lo_ready")
        tanh_g_ready = sem("tanh_g_ready")
        silu2_ready = sem("silu2_ready")
        hidden_ready = sem("hidden_ready")
        h_hi_ready = sem("h_hi_ready")
        h_lo_ready = sem("h_lo_ready")
        result_ready = sem("result_ready")

        def tile_of(b):
            if isinstance(b, int):
                return x_all[:, b, :]
            return x_all[:, bass.ds(b, 1), :].rearrange("p a d -> p (a d)")

        def dram_tile(t, b):
            if isinstance(b, int):
                return t[b]
            return t[bass.ds(b, 1)].rearrange("a s d -> (a s) d")

        def head_view(n, part):
            per, first, count = ((3, 0, 8), (2, 24, 4))[part]
            return bass.AP(v_blocks, (n * H + first) * BLOCK,
                           [[2 * H * BLOCK, P], [per * BLOCK, count], [BLOCK + SLOTW, per], [1, HD]])

        def run(eng, iteration):
            for p in range(FIRST, FIRST_STEADY):
                iteration(p)
            if LOOP:
                with eng.Fori(FIRST_STEADY, LAST_STEADY + 1) as p:
                    iteration(p)
            else:
                for p in range(FIRST_STEADY, LAST_STEADY + 1):
                    iteration(p)
            for p in range(LAST_STEADY + 1, PAIRS + 2):
                iteration(p)

        def here(p, task):
            return exists(p, task) if isinstance(p, int) else True

        def has_tile(p, b):
            return 0 <= b < B if isinstance(p, int) else True

        block = stack.enter_context(nc.Block())

        @block.sync
        def _(sp):
            sp.dma_start(w_raw[:, 0, :, :], Wq.rearrange("(c p) d -> p c d", p=P)).then_inc(w_loaded, 16)
            for c, w in enumerate((Wk, Wv)):
                both = w.rearrange("(p two) d -> p two d", two=2)
                sp.dma_start(w_raw[:, 1:3, c, :], both).then_inc(w_loaded, 16)
            sp.dma_start(x_all[:, 0, :], x[0]).then_inc(x_loaded[0], 16)
            sp.dma_start(ctx_sb[:, 0, :], ctx[0]).then_inc(ctx_loaded[0], 16)
            sp.dma_start(x_all[:, 1, :], x[1]).then_inc(x_loaded[1], 16)
            sp.dma_start(ctx_sb[:, 1, :], ctx[1]).then_inc(ctx_loaded[1], 16)
            sp.dma_start(gates[:, 0:1], g_xattn.rearrange("(a d) -> a d", a=1).to_broadcast([P, 1])).then_inc(small_loaded, 16)
            sp.dma_start(gates[:, 1:2], g_ffn.rearrange("(a d) -> a d", a=1).to_broadcast([P, 1])).then_inc(small_loaded, 16)
            sp.dma_start(down_scale[:], s_down.rearrange("(a d) -> a d", a=1).to_broadcast([P, D])).then_inc(small_loaded, 16)
            full = (NJ - 1) * P
            for k, s in enumerate((s_gate, s_up)):
                with nc.allow_non_contiguous_dma(reason="704 scales, one to a partition"):
                    sp.dma_start(scales[:, k, 0:NJ - 1], s[0:full].rearrange("(j p) -> p j", p=P)).then_inc(small_loaded, 16)
                sp.dma_start(scales[0:LAST, k, NJ - 1:NJ], s[full:HID].rearrange("(p j) -> p j", j=1)).then_inc(small_loaded, 16)
            for k, w in enumerate((wq_gate, wq_up)):
                sp.dma_start(gu_int[:, k, 0:NJ - 1, :], w[0:full, :].rearrange("(j p) d -> p j d", p=P)).then_inc(ffn_w_loaded, 16)
                sp.dma_start(gu_int[0:LAST, k, NJ - 1, :], w[full:HID, :]).then_inc(ffn_w_loaded, 16)
            sp.dma_start(dn_int[:], wq_down.rearrange("(c p) h -> p c h", p=P)).then_inc(ffn_w_loaded, 16)
            sp.dma_start(x_all[:, 2:B, :], x[2:B].rearrange("b p d -> p b d")).then_inc(x_loaded[2], 16)

            def iteration(p):
                for e in range(2):
                    b = 2 * p + e
                    if has_tile(p, b + 1):
                        n = 1 - e
                        k, m = use(p, f"stackk{e}")
                        sp.wait_ge(drained[k], m)
                        if not since(b, 1):
                            sp.wait_ge(km_zeroed, 1)
                        for j in range(4):
                            sp.dma_start(k_masked[BLOCK * j:BLOCK * (j + 1), n, j, :, :],
                                         k_stack[BLOCK * j:BLOCK * (j + 1), n, :, :]).then_inc(km_loaded[n], 16)
                    if has_tile(p, b + 2) and has_tile(p, b + 4):
                        sp.wait_ge(ctx_turned, b + 3)
                        sp.dma_start(ctx_sb[:, e, :], dram_tile(ctx, b + 4)).then_inc(ctx_loaded[e], 16)
                    if e == 0 and (not isinstance(p, int) or p >= 2):
                        for k in range(2):
                            done = 2 * (p - 2) + k
                            sp.wait_ge(result_ready, done + 1)
                            sp.dma_start(dram_tile(out, done), tile_of(done)).then_inc(stored, 16)

            for p in range(FIRST, FIRST_STEADY):
                iteration(p)
            if LOOP:
                with sp.Fori(FIRST_STEADY, PAIRS - 2) as p:
                    iteration(p)
            else:
                for p in range(FIRST_STEADY, PAIRS - 2):
                    iteration(p)
            for p in range(PAIRS - 2, PAIRS + 2):
                iteration(p)
            sp.wait_ge(stored, 16 * B)

        @block.gpsimd
        def _(pool):
            nc.gpsimd.memset(ident[:], 0.0).then_inc(ident_zeroed, 1)
            pool.wait_ge(ident_zeroed, 1)
            nc.gpsimd.affine_select(out=ident[:], in_=ident[:], compare_op=ALU.not_equal, fill=1.0, base=0,
                                    pattern=[[-1, P]], channel_multiplier=1).then_inc(ident_ready, 1)
            pool.wait_ge(ident_ready, 1)
            nc.gpsimd.tensor_copy(ident16[:], ident[:]).then_inc(ident16_ready, 1)
            nc.gpsimd.memset(k_masked[:].bitcast(F32), 0.0).then_inc(km_zeroed, 1)
            nc.gpsimd.memset(v_blocks[:], 0.0).then_inc(v_zeroed, 1)
            pool.wait_ge(v_zeroed, 1)
            for e in range(2):
                v = v_blocks[:, e, 0:24 * BLOCK].rearrange("p (t c) -> p t c", c=3 * BLOCK)
                for i in range(3):
                    nc.gpsimd.memset(v[:, :, i * (BLOCK + SLOTW) + HD:i * (BLOCK + SLOTW) + HD + 1], 1.0)
                w = v_blocks[:, e, 24 * BLOCK:].rearrange("p (t c) -> p t c", c=2 * BLOCK)
                for i in range(2):
                    nc.gpsimd.memset(w[:, :, i * (BLOCK + SLOTW) + HD:i * (BLOCK + SLOTW) + HD + 1], 1.0)
                last = nc.gpsimd.memset(w[:, :, 3 * SLOTW - 1:3 * SLOTW], 1.0)
            last.then_inc(v_ready_ones, 1)
            def split_qk(p, e):
                b = 2 * p + e
                if not has_tile(p, b + 2):
                    return
                pool.wait_ge(qk_hi_ready, b + 3)
                nc.gpsimd.tensor_tensor(qk_parts[:, :, 1, :], qk_unit[:], qk_parts[:, :, 0, :],
                                        ALU.subtract).then_inc(qk_lo_ready, 1)

            def split_hidden(p, q, j):
                n = NJ * (p - q) + j
                pool.wait_ge(h_hi_ready, n + 1)
                r = rows(j)
                nc.gpsimd.tensor_tensor(h_lo[0:r, j, :], hidden[0:r, j % 2, :], h_hi[0:r, j, :].bitcast(F32),
                                        ALU.subtract).then_inc(h_lo_ready, 1)

            def add_y(p, e):
                done = 2 * (p - 2) + e
                k, n = use(p, f"y{e}")
                pool.wait_ge(drained[k], n)
                nc.gpsimd.tensor_tensor(tile_of(done), tile_of(done), y_scaled[:, e, :], ALU.add).then_inc(result_ready, 1)

            def real(p, task):
                return here(p, task) and not (isinstance(p, int) and p == 0)

            def iteration(p):
                if real(p, "ffn3"):
                    split_hidden(p, 2, 3)
                    split_hidden(p, 2, 4)
                    split_hidden(p, 2, 5)
                split_qk(p, 0)
                if real(p, "y0"):
                    add_y(p, 0)
                    add_y(p, 1)
                if real(p, "ffn0"):
                    split_hidden(p, 1, 0)
                split_qk(p, 1)
                if real(p, "ffn0"):
                    split_hidden(p, 1, 1)
                    split_hidden(p, 1, 2)

            run(pool, iteration)

        @block.scalar
        def _(act):
            for m in range(3):
                act.wait_ge(w_turned, m + 1)
                nc.scalar.copy(w_hi[:, :, m * D:(m + 1) * D],
                               score_ps[m % 2][:, 0:4, :].rearrange("p (k a) n -> p k (a n)", k=KC)
                               ).then_inc(w_hi_ready, 1)
            act.wait_ge(small_loaded, 16 * 7)
            nc.scalar.activation(tanh_gates[:], gates[:], ACT.Tanh).then_inc(tanh_ready, 1)

            def exp_octet(p, e, t):
                b = 2 * p + e
                o = OCTETS * b + t
                if not has_tile(p, b):
                    return
                act.wait_ge(scores_ready, o + 1)
                if since(o, 2):
                    act.wait_ge(pv_done, o - 1)
                nc.scalar.activation(probs[:, t % 2, :], score_ps[t % 2][:].rearrange("p h n -> p (h n)"),
                                     ACT.Exp, scale=float(HD) ** 0.5).then_inc(probs_ready, 1)

            def drain_pv(p, e):
                b = 2 * p + e
                if has_tile(p, b - 1):
                    act.wait_ge(pv_done, OCTETS * b)
                    nc.scalar.copy(o_turned[:, 1 - e, :], pv_ps[:, 0:3 * P]).then_inc(o_turned_ready, 1)

            def drain_v(p, e):
                b = 2 * p + e
                if not has_tile(p, b + 1):
                    return
                n = 1 - e
                k, m = use(p, f"v{e}")
                act.wait_ge(filled[k], m)
                if not since(b, 0):
                    act.wait_ge(v_ready_ones, 1)
                src = bank[k][:, 0:24 * HD].rearrange("p (t i d) -> p t i d", i=3, d=HD)
                nc.scalar.copy(head_view(n, 0), src)
                src = bank[k][:, 24 * HD:D].rearrange("p (t i d) -> p t i d", i=2, d=HD)
                nc.scalar.copy(head_view(n, 1), src).then_inc(drained[k], 1)

            def turn_hi(p, e):
                b = 2 * p + e
                if has_tile(p, b + 2):
                    k, m = use(p, f"turn{e}")
                    act.wait_ge(filled[k], m)
                    nc.scalar.copy(xc_hi[:, e, :, :].rearrange("p a n -> p (a n)"), bank[k][:]).then_inc(xc_hi_ready, 1)

            def stack_keys(p, e):
                b = 2 * p + e
                if has_tile(p, b + 1):
                    k, m = use(p, f"stackk{e}")
                    act.wait_ge(filled[k], m)
                    nc.scalar.copy(k_stack[:, 1 - e, :, :].rearrange("p g n -> p (g n)"),
                                   bank[k][:].bitcast(F16)).then_inc(drained[k], 1)

            def square(p, e):
                b = 2 * p + e
                if has_tile(p, b + 2):
                    k, m = use(p, f"qk{e}")
                    act.wait_ge(filled[k], m)
                    if since(b, -1):
                        act.wait_ge(sums_ready, b + 2)
                    nc.scalar.activation(squares[:], bank[k][:], ACT.Square).then_inc(squares_ready, 1)

            def tanh_chunk(p, q, j):
                task = f"ffn{j}"
                if not here(p, task):
                    return
                k, m = use(p, task)
                if isinstance(p, int) and p == 0:
                    prep(task, k, m)
                    return
                n = NJ * (p - q) + j
                act.wait_ge(filled[k], m)
                if since(n, 2):
                    act.wait_ge(silu2_ready, n - 1)
                r = rows(j)
                nc.scalar.activation(tanh_g[0:r, j % 2, :], bank[k][0:r, 0:TOK], ACT.Tanh,
                                     scale=half_gate[0:r, j:j + 1]).then_inc(tanh_g_ready, 1)

            def prep(task, k, m):
                part = PREP[task]
                act.wait_ge(filled[k], m)
                if part < NJ:
                    nc.scalar.copy(gu_hi[:, part, :, :, 0:rows(part)],
                                   bank[k][:].rearrange("p (a c n) -> p a c n", a=2, c=KC)[:, :, :, 0:rows(part)]
                                   ).then_inc(prep_hi, 1)
                    return
                for a in range(2):
                    j = 2 * (part - NJ) + a
                    last = nc.scalar.copy(dn_hi[0:rows(j), j, :], bank[k][0:rows(j), a * D:(a + 1) * D])
                last.then_inc(prep_hi, 1)

            def turn2_hi(p):
                if not here(p, "turn2"):
                    return
                k, m = use(p, "turn2")
                if isinstance(p, int) and p == 0:
                    prep("turn2", k, m)
                    return
                act.wait_ge(filled[k], m)
                nc.scalar.copy(x2_hi[:].rearrange("p c n -> p (c n)"), bank[k][:]).then_inc(x2_hi_ready, 1)

            def iteration(p):
                first = isinstance(p, int) and p == 0
                if first:
                    act.wait_ge(scale_steps, 2)
                exp_octet(p, 0, 0)
                drain_pv(p, 0)
                turn_hi(p, 0)
                tanh_chunk(p, 2, 3)
                tanh_chunk(p, 2, 4)
                exp_octet(p, 0, 1)
                stack_keys(p, 0)
                square(p, 0)
                exp_octet(p, 0, 2)
                drain_v(p, 0)
                tanh_chunk(p, 2, 5)
                exp_octet(p, 0, 3)
                if first:
                    prep("y0", *use(p, "y0"))
                exp_octet(p, 1, 0)
                drain_pv(p, 1)
                turn_hi(p, 1)
                turn2_hi(p)
                if first:
                    prep("y1", *use(p, "y1"))
                exp_octet(p, 1, 1)
                stack_keys(p, 1)
                square(p, 1)
                exp_octet(p, 1, 2)
                drain_v(p, 1)
                tanh_chunk(p, 1, 0)
                exp_octet(p, 1, 3)
                tanh_chunk(p, 1, 1)
                tanh_chunk(p, 1, 2)

            run(act, iteration)

        @block.vector
        def _(dve):
            nc.vector.memset(mean_var[:], 1.0)
            nc.vector.memset(root_in[:], 1.0)
            for m in range(3):
                dve.wait_ge(w_hi_ready, m + 1)
                nc.vector.tensor_tensor(w_lo[:, :, m * D:(m + 1) * D],
                                        score_ps[m % 2][:, 0:4, :].rearrange("p (k a) n -> p k (a n)", k=KC),
                                        w_hi[:, :, m * D:(m + 1) * D].bitcast(F32), ALU.subtract).then_inc(w_lo_ready, 1)

            def statistics(p, e):
                b = 2 * p + e + 3
                if not has_tile(p, b):
                    return
                if isinstance(b, int) and b <= 2:
                    dve.wait_ge(x_loaded[b], 16)
                nc.vector.bn_stats(stats[:, 0, :], tile_of(b)).then_inc(stats_ready, 1)

            def mean(p, e):
                b = 2 * p + e + 3
                if has_tile(p, b):
                    dve.wait_ge(stats_ready, b + 1)
                    nc.vector.bn_aggr(mean_var[:, 0, :], stats[:, 0, :]).then_inc(mean_ready, 1)

            def mean2(p, e):
                b = 2 * p + e - 1
                if has_tile(p, b):
                    dve.wait_ge(stats2_ready, b + 1)
                    nc.vector.bn_aggr(mean_var[:, 1, :], stats[:, 1, :]).then_inc(mean2_ready, 1)

            def has_roots(p, b):
                return -3 <= b <= B if isinstance(p, int) else True

            def root_inputs(p, e):
                b = 2 * p + e
                if not has_roots(p, b):
                    return
                if has_tile(p, b + 2):
                    dve.wait_ge(sums_ready, b + 3)
                    nc.vector.tensor_scalar(root_in[:, 0:2 * H], sums[:], HD * RMS_EPS, None, ALU.add)
                if has_tile(p, b + 3):
                    dve.wait_ge(mean_ready, b + 4)
                if has_tile(p, b - 1):
                    dve.wait_ge(mean2_ready, b)
                nc.vector.tensor_scalar(root_in[:, 2 * H:], mean_var[:, :, 1], LN_EPS, None,
                                        ALU.add).then_inc(root_in_ready, 1)

            def root(p, e, first, last):
                b = 2 * p + e
                if not has_roots(p, b):
                    return
                for step in range(first, last):
                    if step == 0:
                        dve.wait_ge(root_in_ready, b + 4)
                        bits = nc.vector.tensor_scalar(root_y[:].bitcast(I32), root_in[:].bitcast(I32), -0.5, START_BITS, ALU.mult, ALU.add)
                        bits.then_inc(root_steps, 1)
                        continue
                    dve.wait_ge(root_steps, RSQRT_STEPS * (b + 3) + step)
                    scale = START_SCALE if step <= 4 else MID_SCALE
                    k = (step - 1) % 4
                    if k == 0:
                        ins = nc.vector.tensor_tensor(root_xy[:], root_in[:], root_y[:], ALU.mult)
                    elif k == 1:
                        ins = nc.vector.tensor_tensor(root_v[:], root_xy[:], root_y[:], ALU.mult)
                    elif k == 2:
                        ins = nc.vector.scalar_tensor_tensor(out=root_p[:], in0=root_v[:], scalar=-10 / 3 * scale ** 2,
                                                             in1=root_v[:], op0=ALU.add, op1=ALU.mult)
                    else:
                        ins = nc.vector.scalar_tensor_tensor(out=root_y[:], in0=root_p[:], scalar=5 * scale ** 4,
                                                             in1=root_y[:], op0=ALU.add, op1=ALU.mult)
                    ins.then_inc(root_steps, 1)

            def normalize(p, e):
                b = 2 * p + e + 3
                if has_tile(p, b):
                    dve.wait_ge(root_steps, RSQRT_STEPS * (b + 1))
                    nc.vector.tensor_scalar(xn[:, 1 - e, :], tile_of(b), mean_var[:, 0, 0:1], root_y[:, 2 * H:2 * H + 1],
                                            ALU.subtract, ALU.mult).then_inc(xn_ready, 1)

            def normalize2(p, e):
                b = 2 * p + e - 1
                if has_tile(p, b):
                    dve.wait_ge(root_steps, RSQRT_STEPS * (b + 5))
                    nc.vector.tensor_scalar(x1n[:, 1 - e, :], tile_of(b), mean_var[:, 1, 0:1], root_y[:, 2 * H + 1:2 * H + 2],
                                            ALU.subtract, ALU.mult).then_inc(x1n_ready, 1)

            def turn_lo(p, e):
                b = 2 * p + e
                if has_tile(p, b + 2):
                    k, m = use(p, f"turn{e}")
                    dve.wait_ge(filled[k], m)
                    dve.wait_ge(xc_hi_ready, b + 3)
                    nc.vector.tensor_tensor(xc_lo[:, e, :, :].rearrange("p a n -> p (a n)"), bank[k][:],
                                            xc_hi[:, e, :, :].rearrange("p a n -> p (a n)").bitcast(F32),
                                            ALU.subtract).then_inc(drained[k], 1)

            def sum_squares(p, e):
                b = 2 * p + e
                if has_tile(p, b + 2):
                    dve.wait_ge(squares_ready, b + 3)
                    nc.vector.tensor_reduce(sums[:], squares[:].rearrange("p (h d) -> p h d", d=HD), AX.X,
                                            ALU.add).then_inc(sums_ready, 1)

            def qk_norm(p, e):
                b = 2 * p + e
                if not has_tile(p, b + 2):
                    return
                k, m = use(p, f"qk{e}")
                dve.wait_ge(root_steps, RSQRT_STEPS * (b + 4))
                if since(b, -1):
                    dve.wait_ge(qk_lo_ready, b + 2)
                nc.vector.tensor_tensor(qk_unit[:], bank[k][:].rearrange("p (h d) -> p h d", d=HD),
                                        root_y[:, 0:2 * H].unsqueeze(2).to_broadcast([P, 2 * H, HD]),
                                        ALU.mult).then_inc(drained[k], 1)

            def qk_upper(p, e):
                b = 2 * p + e
                if not has_tile(p, b + 2):
                    return
                k, m = use(p, f"qk{e}")
                dve.wait_ge(drained[k], m)
                if since(b, -1):
                    k, m = use(p, f"stackk{e}")
                    dve.wait_ge(filled[k], m)
                nc.vector.tensor_copy(qk_parts[:, :, 0, :], qk_unit[:]).then_inc(qk_hi_ready, 1)

            def qk_double(p, e):
                b = 2 * p + e
                if not has_tile(p, b + 1):
                    return
                dve.wait_ge(qk_lo_ready, b + 2)
                words = qk_parts[:].rearrange("p h a d -> p h (a d)").bitcast(F32)
                W = HD // 2
                nc.vector.tensor_copy(words[:, 0:H, 2 * W:4 * W], words[:, 0:H, 0:2 * W])
                nc.vector.tensor_copy(words[:, H:2 * H, 2 * W:3 * W], words[:, H:2 * H, W:2 * W])
                nc.vector.tensor_copy(words[:, H:2 * H, 3 * W:4 * W], words[:, H:2 * H, 0:W]).then_inc(qk_parts_ready, 1)

            def stack_queries(p, e):
                b = 2 * p + e
                if has_tile(p, b + 1):
                    k, m = use(p, f"stackq{e}")
                    dve.wait_ge(filled[k], m)
                    nc.vector.tensor_copy(q_stack[:, 1 - e, :, :].rearrange("p g n -> p (g n)"),
                                          bank[k][:].bitcast(F16)).then_inc(drained[k], 1)

            def out_reciprocal(p, e):
                b = 2 * p + e - 1
                if has_tile(p, b):
                    k, m = use(p, f"out{e}")
                    dve.wait_ge(filled[k], m)
                    nc.vector.reciprocal(inv_den[:], out_slots(k)[:, :, :, HD]).then_inc(inv_den_ready, 1)

            def out_slots(k):
                blocks = bank[k][:, 0:3 * P].rearrange("p (t c) -> p t c", c=BLOCK)
                return blocks[:, :, 0:3 * SLOTW].rearrange("p t (i c) -> p t i c", c=SLOTW)

            def out_divide(p, e):
                b = 2 * p + e - 1
                if not has_tile(p, b):
                    return
                k, m = use(p, f"out{e}")
                dve.wait_ge(inv_den_ready, b + 1)
                for t0, t1, per, h0 in ((0, 8, 3, 0), (8, 12, 2, 24)):
                    dst = attn[:, h0 * HD:(h0 + (t1 - t0) * per) * HD].rearrange("p (t i d) -> p t i d", i=per, d=HD)
                    last = nc.vector.tensor_tensor(dst, out_slots(k)[:, t0:t1, 0:per, 0:HD],
                                                   inv_den[:, t0:t1, 0:per].unsqueeze(3).to_broadcast([P, t1 - t0, per, HD]),
                                                   ALU.mult)
                    if t0 == 0:
                        last.then_inc(attn_ready, 1)
                last.then_inc(drained[k], 1)

            def add_attention(p, e):
                b = 2 * p + e - 1
                if not has_tile(p, b):
                    return
                k, m = use(p, f"out{e}")
                dve.wait_ge(attn_ready, b + 1)
                dve.wait_ge(drained[k], m)
                nc.vector.scalar_tensor_tensor(out=tile_of(b), in0=attn[:], scalar=tanh_gates[:, 0:1], in1=tile_of(b),
                                               op0=ALU.mult, op1=ALU.add).then_inc(x1_ready, 1)

            def statistics2(p, e):
                b = 2 * p + e - 1
                if has_tile(p, b):
                    dve.wait_ge(x1_ready, b + 1)
                    nc.vector.bn_stats(stats[:, 1, :], tile_of(b)).then_inc(stats2_ready, 1)

            def gate(p, q, j):
                task = f"ffn{j}"
                if not here(p, task):
                    return
                k, m = use(p, task)
                if isinstance(p, int) and p == 0:
                    prep(task, k, m)
                    return
                n = NJ * (p - q) + j
                r = rows(j)
                if isinstance(n, int) and n == 0:
                    dve.wait_ge(scale_steps, 5)
                dve.wait_ge(tanh_g_ready, n + 1)
                nc.vector.scalar_tensor_tensor(out=silu2[0:r, j % 2, :], in0=tanh_g[0:r, j % 2, :], scalar=1.0,
                                               in1=bank[k][0:r, 0:TOK], op0=ALU.add, op1=ALU.mult).then_inc(silu2_ready, 1)

            def up(p, q, j):
                task = f"ffn{j}"
                if not here(p, task) or isinstance(p, int) and p == 0:
                    return
                k, m = use(p, task)
                n = NJ * (p - q) + j
                r = rows(j)
                dve.wait_ge(silu2_ready, n + 1)
                if since(n, 2):
                    dve.wait_ge(h_lo_ready, n - 1)
                nc.vector.scalar_tensor_tensor(out=hidden[0:r, j % 2, :], in0=silu2[0:r, j % 2, :], scalar=scales[0:r, 2, j:j + 1],
                                               in1=bank[k][0:r, TOK:2 * TOK], op0=ALU.mult, op1=ALU.mult).then_inc(drained[k], 1)

            def upper(p, q, j):
                task = f"ffn{j}"
                if not here(p, task) or isinstance(p, int) and p == 0:
                    return
                k, m = use(p, task)
                r = rows(j)
                dve.wait_ge(drained[k], m)
                nc.vector.tensor_copy(h_hi[0:r, j, :], hidden[0:r, j % 2, :]).then_inc(h_hi_ready, 1)

            def prep(task, k, m):
                part = PREP[task]
                dve.wait_ge(filled[k], m)
                dve.wait_ge(prep_hi, part + 1)
                if part < NJ:
                    r = rows(part)
                    nc.vector.tensor_tensor(gu_lo[:, part, :, :, 0:r],
                                            bank[k][:].rearrange("p (a c n) -> p a c n", a=2, c=KC)[:, :, :, 0:r],
                                            gu_hi[:, part, :, :, 0:r].bitcast(F32), ALU.subtract).then_inc(drained[k], 1)
                    return
                for a in range(2):
                    j = 2 * (part - NJ) + a
                    last = nc.vector.tensor_tensor(dn_lo[0:rows(j), j, :], bank[k][0:rows(j), a * D:(a + 1) * D],
                                                   dn_hi[0:rows(j), j, :].bitcast(F32), ALU.subtract)
                last.then_inc(drained[k], 1)

            def turn2_lo(p):
                if not here(p, "turn2"):
                    return
                k, m = use(p, "turn2")
                if isinstance(p, int) and p == 0:
                    prep("turn2", k, m)
                    return
                dve.wait_ge(filled[k], m)
                dve.wait_ge(x2_hi_ready, p)
                nc.vector.tensor_tensor(x2_lo[:].rearrange("p c n -> p (c n)"), bank[k][:],
                                        x2_hi[:].rearrange("p c n -> p (c n)").bitcast(F32),
                                        ALU.subtract).then_inc(drained[k], 1)

            def scale_y(p, e):
                task = f"y{e}"
                if not here(p, task):
                    return
                k, m = use(p, task)
                if isinstance(p, int) and p == 0:
                    prep(task, k, m)
                    return
                done = 2 * (p - 2) + e
                dve.wait_ge(filled[k], m)
                if since(done, 2):
                    dve.wait_ge(result_ready, done - 1)
                nc.vector.tensor_tensor(y_scaled[:, e, :], bank[k][:, 0:D], down_scale[:], ALU.mult).then_inc(drained[k], 1)

            def scale_setup():
                dve.wait_ge(small_loaded, 16 * 7)
                for r, j0, j1 in ((P, 0, NJ - 1), (LAST, NJ - 1, NJ)):
                    nc.vector.tensor_scalar(half_gate[0:r, j0:j1], scales[0:r, 0, j0:j1], 0.5, None, ALU.mult).then_inc(scale_steps, 1)
                dve.wait_ge(scale_steps, 2)
                for r, j0, j1 in ((P, 0, NJ - 1), (LAST, NJ - 1, NJ)):
                    nc.vector.tensor_tensor(scales[0:r, 2, j0:j1], half_gate[0:r, j0:j1], scales[0:r, 1, j0:j1],
                                            ALU.mult).then_inc(scale_steps, 1)
                dve.wait_ge(tanh_ready, 1)
                nc.vector.tensor_scalar(down_scale[:], down_scale[:], tanh_gates[:, 1:2], None, ALU.mult).then_inc(scale_steps, 1)

            def convert_weights():
                dve.wait_ge(ffn_w_loaded, 16 * 5)
                for k in range(2):
                    nc.vector.tensor_scalar(gu_raw[:, k, 0:NJ - 1, :], gu_int[:, k, 0:NJ - 1, :], -ZERO_POINT, None, ALU.add)
                    nc.vector.tensor_scalar(gu_raw[0:LAST, k, NJ - 1, :], gu_int[0:LAST, k, NJ - 1, :], -ZERO_POINT, None, ALU.add)
                nc.vector.tensor_scalar(dn_raw[:], dn_int[:], -ZERO_POINT, None, ALU.add).then_inc(w_converted, 1)

            def iteration(p):
                turn_lo(p, 0)
                qk_double(p, 0)
                gate(p, 2, 3)
                statistics(p, 0)
                up(p, 2, 3)
                mean(p, 0)
                gate(p, 2, 4)
                upper(p, 2, 3)
                up(p, 2, 4)
                out_reciprocal(p, 0)
                upper(p, 2, 4)
                stack_queries(p, 0)
                out_divide(p, 0)
                sum_squares(p, 0)
                add_attention(p, 0)
                statistics2(p, 0)
                mean2(p, 0)
                root_inputs(p, 0)
                root(p, 0, 0, 1)
                gate(p, 2, 5)
                root(p, 0, 1, 2)
                up(p, 2, 5)
                root(p, 0, 2, 3)
                upper(p, 2, 5)
                root(p, 0, 3, 9)
                qk_norm(p, 0)
                normalize2(p, 0)
                qk_upper(p, 0)
                normalize(p, 0)
                scale_y(p, 0)
                turn_lo(p, 1)
                qk_double(p, 1)
                statistics(p, 1)
                turn2_lo(p)
                mean(p, 1)
                scale_y(p, 1)
                out_reciprocal(p, 1)
                stack_queries(p, 1)
                out_divide(p, 1)
                sum_squares(p, 1)
                add_attention(p, 1)
                statistics2(p, 1)
                mean2(p, 1)
                root_inputs(p, 1)
                root(p, 1, 0, 1)
                gate(p, 1, 0)
                root(p, 1, 1, 2)
                up(p, 1, 0)
                root(p, 1, 2, 3)
                upper(p, 1, 0)
                root(p, 1, 3, 9)
                qk_norm(p, 1)
                normalize2(p, 1)
                qk_upper(p, 1)
                normalize(p, 1)
                gate(p, 1, 1)
                up(p, 1, 1)
                gate(p, 1, 2)
                upper(p, 1, 1)
                up(p, 1, 2)
                upper(p, 1, 2)
                if isinstance(p, int) and p == -1:
                    scale_setup()
                    convert_weights()

            run(dve, iteration)

        @block.tensor
        def _(pe):
            pe.wait_ge(ident_ready, 1)
            pe.wait_ge(w_loaded, 16 * 3)
            for m in range(3):
                if m == 2:
                    pe.wait_ge(w_lo_ready, 1)
                for k in range(KC):
                    for c in range(KC):
                        last = nc.tensor.transpose(score_ps[m % 2][:, KC * k + c, :], w_raw[:, m, c, k * P:(k + 1) * P], ident[:])
                last.then_inc(w_turned, 1)

            def claim(p, task):
                k, m = use(p, task)
                if since(m, 2):
                    pe.wait_ge(drained[k], m - 1)
                return k

            def scores(p, e, t):
                b = 2 * p + e
                if not has_tile(p, b):
                    return
                o = OCTETS * b + t
                if t == 0:
                    k, m = use(p, "stackq0") if e else use(p - 1, "stackq1")
                    pe.wait_ge(drained[k], m)
                    pe.wait_ge(km_loaded[e], 64 * (p + 1))
                if isinstance(o, int) and o == 0:
                    pe.wait_ge(w_lo_ready, 3)
                if since(o, 2):
                    pe.wait_ge(probs_ready, o - 1)
                for s in range(HEADS_PER_OCTET):
                    h = place(HEADS_PER_OCTET * t + s)[0]
                    last = nc.tensor.matmul(score_ps[t % 2][:, s, :], k_masked[:, e, h % 4, h // 4, :],
                                            q_stack[:, e, h // 4, :], start=True, stop=True)
                last.then_inc(scores_ready, 1)

            def weigh(p, e, t):
                b = 2 * p + e
                o = OCTETS * b + t - 1
                e, t = (e, t - 1) if t else (1 - e, OCTETS - 1)
                b = b if t < OCTETS - 1 else b - 1
                if not has_tile(p, b):
                    return
                pe.wait_ge(probs_ready, o + 1)
                if t == 0:
                    pe.wait_ge(v_ready_of(p, b, e)[0], v_ready_of(p, b, e)[1])
                    if since(b, 1):
                        pe.wait_ge(o_turned_ready, b)
                for s in range(HEADS_PER_OCTET):
                    h, region, quadrant, i = place(HEADS_PER_OCTET * t + s)
                    last = nc.tensor.matmul(pv_ps[BLOCK * quadrant:BLOCK * (quadrant + 1), region * P:(region + 1) * P],
                                            v_blocks[:, e, h * BLOCK:(h + 1) * BLOCK],
                                            probs[:, t % 2, s * P:(s + 1) * P],
                                            start=(i == 0), stop=(i == (2 if region < 2 else 1)),
                                            tile_position=(0, BLOCK * quadrant))
                last.then_inc(pv_done, 1)

            def v_ready_of(p, b, e):
                if e == 0:
                    k, m = use(p - 1, "v1")
                    return drained[k], m
                k, m = use(p, "v0")
                return drained[k], m

            def turn(p, e):
                b = 2 * p + e
                if not has_tile(p, b + 2):
                    return
                k = claim(p, f"turn{e}")
                pe.wait_ge(ctx_loaded[e], 16 * (p + 2))
                for c in range(KC):
                    last = nc.tensor.transpose(bank[k][:, (KC + c) * P:(KC + c + 1) * P], ctx_sb[:, e, c * P:(c + 1) * P], ident[:])
                last.then_inc(ctx_turned, 1)
                pe.wait_ge(xn_ready, b + 3)
                for c in range(KC):
                    last = nc.tensor.transpose(bank[k][:, c * P:(c + 1) * P], xn[:, e, c * P:(c + 1) * P], ident[:])
                last.then_inc(filled[k], 1)

            def project(dst, tile, source, column):
                n = 0
                for c in range(KC):
                    for a, w in ((xc_hi, w_hi), (xc_hi, w_lo), (xc_lo, w_hi)):
                        n += 1
                        last = nc.tensor.matmul(dst, a[:, tile, KC * source + c, :], w[:, c, column * D:(column + 1) * D],
                                                start=(n == 1), stop=(n == 3 * KC))
                return last

            def queries_keys(p, e):
                b = 2 * p + e
                if not has_tile(p, b + 2):
                    return
                k = claim(p, f"qk{e}")
                j, m = use(p, f"turn{e}")
                pe.wait_ge(drained[j], m)
                if isinstance(b, int) and b == -2:
                    pe.wait_ge(w_lo_ready, 3)
                project(bank[k][:, 0:D], e, 0, 0)
                project(bank[k][:, D:2 * D], e, 1, 1).then_inc(filled[k], 1)

            def values(p, e):
                b = 2 * p + e
                if not has_tile(p, b + 1):
                    return
                k = claim(p, f"v{e}")
                project(bank[k][:, 0:D], 1 - e, 1, 2).then_inc(filled[k], 1)

            def stacks(p, e):
                b = 2 * p + e
                if not has_tile(p, b + 1):
                    return
                if isinstance(b, int) and b == -1:
                    pe.wait_ge(ident16_ready, 1)
                for name in ("stackq", "stackk"):
                    k = claim(p, f"{name}{e}")
                    if name == "stackq":
                        pe.wait_ge(qk_parts_ready, b + 2)
                    dst = bank[k][:].bitcast(F16)
                    for g in range(GROUPS):
                        h = 4 * g + (0 if name == "stackq" else H)
                        src = qk_parts[:, h:h + 4, :, :].rearrange("p h a d -> p (h a d)")
                        last = nc.tensor.transpose(dst[:, g * P:(g + 1) * P], src, ident16[:])
                    last.then_inc(filled[k], 1)

            def out_rows(p, e):
                b = 2 * p + e
                if not has_tile(p, b - 1):
                    return
                k = claim(p, f"out{e}")
                pe.wait_ge(o_turned_ready, b)
                for r in range(3):
                    last = nc.tensor.transpose(bank[k][:, r * P:(r + 1) * P], o_turned[:, 1 - e, r * P:(r + 1) * P], ident[:])
                last.then_inc(filled[k], 1)

            def prep(task):
                part = PREP[task]
                k = claim(0, task)
                pe.wait_ge(w_converted, 1)
                if part < NJ:
                    r = rows(part)
                    for a in range(2):
                        for c in range(KC):
                            col = (KC * a + c) * P
                            last = nc.tensor.transpose(bank[k][:, col:col + r], gu_raw[0:r, a, part, c * P:(c + 1) * P], ident[0:r, 0:r])
                else:
                    for a in range(2):
                        j = 2 * (part - NJ) + a
                        for c in range(KC):
                            col = a * D + c * P
                            last = nc.tensor.transpose(bank[k][0:rows(j), col:col + P], dn_raw[:, c, j * P:j * P + rows(j)], ident[:])
                last.then_inc(filled[k], 1)

            def turn2(p):
                if not here(p, "turn2"):
                    return
                if isinstance(p, int) and p == 0:
                    return prep("turn2")
                k = claim(p, "turn2")
                pe.wait_ge(x1n_ready, 2 * p)
                for c in range(KC):
                    for e in range(2):
                        last = nc.tensor.transpose(bank[k][:, c * TOK + e * P:c * TOK + (e + 1) * P], x1n[:, e, c * P:(c + 1) * P], ident[:])
                last.then_inc(filled[k], 1)

            def chunk(p, j):
                task = f"ffn{j}"
                if not here(p, task):
                    return
                if isinstance(p, int) and p == 0:
                    return prep(task)
                k = claim(p, task)
                if j == 0:
                    i, m = use(p, "turn2")
                    pe.wait_ge(drained[i], m)
                r = rows(j)
                for a in range(2):
                    n = 0
                    for c in range(KC):
                        for w, xx in ((gu_hi, x2_hi), (gu_hi, x2_lo), (gu_lo, x2_hi)):
                            n += 1
                            last = nc.tensor.matmul(bank[k][0:r, a * TOK:(a + 1) * TOK], w[:, j, a, c, 0:r], xx[:, c, :],
                                                    start=(n == 1), stop=(n == 3 * KC))
                last.then_inc(filled[k], 1)

            def down(p, e):
                task = f"y{e}"
                if not here(p, task):
                    return
                if isinstance(p, int) and p == 0:
                    return prep(task)
                k = claim(p, task)
                n = 0
                for j in range(NJ):
                    if e == 0 and j >= 3:
                        pe.wait_ge(h_lo_ready, NJ * (p - 2) + j + 1)
                    r = rows(j)
                    for hh, w in ((h_hi, dn_hi), (h_lo, dn_hi), (h_hi, dn_lo)):
                        n += 1
                        last = nc.tensor.matmul(bank[k][:, 0:D], hh[0:r, j, e * P:(e + 1) * P], w[0:r, j, :],
                                                start=(n == 1), stop=(n == 3 * NJ))
                last.then_inc(filled[k], 1)

            def iteration(p):
                scores(p, 0, 0)
                weigh(p, 0, 0)
                turn(p, 0)
                chunk(p, 3)
                chunk(p, 4)

                scores(p, 0, 1)
                out_rows(p, 0)
                stacks(p, 0)
                queries_keys(p, 0)
                weigh(p, 0, 1)

                scores(p, 0, 2)
                values(p, 0)
                chunk(p, 5)
                weigh(p, 0, 2)

                scores(p, 0, 3)
                down(p, 0)
                weigh(p, 0, 3)

                scores(p, 1, 0)
                weigh(p, 1, 0)
                turn(p, 1)
                turn2(p)
                down(p, 1)

                scores(p, 1, 1)
                out_rows(p, 1)
                stacks(p, 1)
                queries_keys(p, 1)
                weigh(p, 1, 1)

                scores(p, 1, 2)
                values(p, 1)
                chunk(p, 0)
                weigh(p, 1, 2)

                scores(p, 1, 3)
                chunk(p, 1)
                chunk(p, 2)
                weigh(p, 1, 3)

            run(pe, iteration)


INPUTS = ["x", "ctx_2048", "g_xattn", "g_ffn", "L0_xattn_Wq", "L0_xattn_Wk", "L0_xattn_Wv", "L0_ffn_wq_gate",
          "L0_ffn_s_gate", "L0_ffn_wq_up", "L0_ffn_s_up", "L0_ffn_wq_down", "L0_ffn_s_down"]


def kernel(**inputs):
    import numpy as np
    import concourse.bacc as bacc
    from concourse.bass_utils import run_bass_kernel_spmd

    nc = bacc.Bacc("TRN2", target_bir_lowering=False, num_devices=1)
    arrays, args = {}, []
    for name in INPUTS:
        a = np.ascontiguousarray(inputs[name])
        arrays[f"{name}_dram"] = a
        args.append(nc.dram_tensor(f"{name}_dram", a.shape, mybir.dt.from_np(a.dtype), kind="ExternalInput").ap())
    x = arrays["x_dram"]
    args.append(nc.dram_tensor("out_dram", x.shape, mybir.dt.from_np(x.dtype), kind="ExternalOutput").ap())
    build_program(nc, *args)
    result = run_bass_kernel_spmd(nc, [arrays], core_ids=[0])
    return result.results[0]["out_dram"]
```

```python
from contextlib import ExitStack

import concourse.bass as bass
from concourse import mybir

ALU = mybir.AluOpType
ACT = mybir.ActivationFunctionType
AX = mybir.AxisListType
F32 = mybir.dt.float32
F32R = mybir.dt.float32r
F16 = mybir.dt.float16
I32 = mybir.dt.int32

P = 128
HD = 8
LN_EPS = 1e-5
RMS_EPS = 1e-6
ZERO_POINT = 128.0

MID_SCALE = 0.375 ** 0.2
START_SCALE = (0.375 * MID_SCALE) ** 0.2
START_BITS = 1594644007.0
RSQRT_STEPS = 9
F32R_INTEGERS = 4096.0
BLOCK = 32
SLOTW = HD + 1
HEADS_PER_OCTET = 8
LOOP = True


def build_program(nc, x, ctx, g_xattn, g_ffn, Wq, Wk, Wv, wq_gate, s_gate, wq_up, s_up, wq_down, s_down, out):
    B, S, D = x.shape
    HID = wq_gate.shape[0]
    H = D // HD
    KC = D // P
    NJ = -(-HID // P)
    LAST = HID - (NJ - 1) * P
    PAIRS = B // 2
    OCTETS = H // HEADS_PER_OCTET
    GROUPS = H // 4
    TOK = 2 * S
    assert S == P and D == 2 * P and H == 32 and B % 2 == 0 and NJ == 6

    def rows(j):
        return P if j < NJ - 1 else LAST

    def place(n):
        region, i, quadrant = (n // 12, n % 12 // 4, n % 4) if n < 24 else (2, (n - 24) // 4, n % 4)
        head = 12 * region + 3 * quadrant + i if region < 2 else 24 + 2 * quadrant + i
        return head, region, quadrant, i

    TASKS = ["turn0", "ffn3", "ffn4", "out0", "stackq0", "stackk0", "qk0", "v0", "ffn5", "y0",
             "turn1", "turn2", "y1", "out1", "stackq1", "stackk1", "qk1", "v1", "ffn0", "ffn1", "ffn2"]
    PREP = {"ffn3": 0, "ffn4": 1, "ffn5": 2, "y0": 3, "turn2": 4, "y1": 5, "ffn0": 6, "ffn1": 7, "ffn2": 8}
    NBANK = 3

    def exists(p, task):
        if task in PREP and p == 0:
            return True
        if task in ("ffn3", "ffn4", "ffn5", "y0", "y1"):
            return 0 <= p - 2 < PAIRS
        if task in ("turn2", "ffn0", "ffn1", "ffn2"):
            return 0 <= p - 1 < PAIRS
        b = 2 * p + int(task[-1])
        ahead = {"out": -1, "sta": 1, "v": 1, "v0": 1, "v1": 1, "tur": 2, "qk0": 2, "qk1": 2}[task[:3]]
        return 0 <= b + ahead < B

    FIRST, FIRST_STEADY, LAST_STEADY = -2, 2, PAIRS - 3

    def use(p, task):
        pos = TASKS.index(task)
        q = p if isinstance(p, int) else FIRST_STEADY
        n = sum(exists(i, t) for i in range(FIRST, q + 1) for k, t in enumerate(TASKS)
                if k % NBANK == pos % NBANK and (i < q or k <= pos))
        return pos % NBANK, n if isinstance(p, int) else n + len(TASKS) // NBANK * (p - FIRST_STEADY)

    def since(v, least):
        return v >= least if isinstance(v, int) else True

    with ExitStack() as stack:
        def sb(name, shape, dt=F32):
            return stack.enter_context(nc.sbuf_tensor(name, shape, dt))

        def sem(name):
            return stack.enter_context(nc.semaphore(name))

        x_all = sb("x_all", [P, B, D])
        ctx_sb = sb("ctx_sb", [P, 2, D])
        w_raw = sb("w_raw", [P, 3, KC, D])
        w_hi = sb("w_hi", [P, KC, 3 * D], F32R)
        w_lo = sb("w_lo", [P, KC, 3 * D], F32R)
        gu_int = sb("gu_int", [P, 2, NJ, D], I32)
        dn_int = sb("dn_int", [P, KC, HID], I32)
        gu_raw = sb("gu_raw", [P, 2, NJ, D])
        dn_raw = sb("dn_raw", [P, KC, HID])
        gu_hi = sb("gu_hi", [P, NJ, 2, KC, P], F32R)
        gu_lo = sb("gu_lo", [P, NJ, 2, KC, P], F32R)
        dn_hi = sb("dn_hi", [P, NJ, D], F32R)
        dn_lo = sb("dn_lo", [P, NJ, D], F32R)
        weight_max = sb("weight_max", [P, 4])
        wide_max = sb("wide_max", [1, 1])
        wide = sb("wide", [1, 1], I32)
        scales = sb("scales", [P, 3, NJ])
        half_gate = sb("half_gate", [P, NJ])
        down_scale = sb("down_scale", [P, D])
        gates = sb("gates", [P, 2])
        tanh_gates = sb("tanh_gates", [P, 2])
        ident = sb("ident", [P, P])
        ident16 = sb("ident16", [P, P], F16)
        stats = sb("stats", [P, 2, 6])
        mean_var = sb("mean_var", [P, 2, 2])
        xn = sb("xn", [P, 2, D])
        x1n = sb("x1n", [P, 2, D])
        norm_bias = sb("norm_bias", [P, 2])
        root_in = sb("root_in", [P, 2 * H + 2])
        root_y = sb("root_y", [P, 2 * H + 2])
        root_xy = sb("root_xy", [P, 2 * H + 2])
        root_v = sb("root_v", [P, 2 * H + 2])
        root_p = sb("root_p", [P, 2 * H + 2])
        xc_hi = sb("xc_hi", [P, 2, 2 * KC, P], F32R)
        xc_lo = sb("xc_lo", [P, 2, 2 * KC, P], F32R)
        squares = sb("squares", [P, 2 * D])
        qk_raw = sb("qk_raw", [P, 2 * H, HD])
        sums = sb("sums", [P, 2 * H])
        qk_unit = sb("qk_unit", [P, 2 * H, HD])
        qk_parts = sb("qk_parts", [P, 2 * H, 4, HD], F16)
        q_stack = sb("q_stack", [P, 2, GROUPS, P], F16)
        k_stack = sb("k_stack", [P, 2, GROUPS, P], F16)
        k_masked = sb("k_masked", [P, 2, 4, GROUPS, P], F16)
        v_blocks = sb("v_blocks", [P, 2, H * BLOCK])
        probs = sb("probs", [P, 2, HEADS_PER_OCTET * P])
        o_turned = sb("o_turned", [P, 2, 3 * P])
        inv_den = sb("inv_den", [P, 12, 3])
        gated_inv = sb("gated_inv", [P, 12, 3])
        attn = sb("attn", [P, D])
        x2_hi = sb("x2_hi", [P, KC, TOK], F32R)
        x2_lo = sb("x2_lo", [P, KC, TOK], F32R)
        tanh_g = sb("tanh_g", [P, 2, TOK])
        silu2 = sb("silu2", [P, 2, TOK])
        hidden = sb("hidden", [P, 2, TOK])
        h_hi = sb("h_hi", [P, NJ, TOK], F32R)
        h_lo = sb("h_lo", [P, NJ, TOK], F32R)
        y_sb = sb("y_sb", [P, 2, D])

        score_ps = [stack.enter_context(nc.psum_tensor(f"score_ps{i}", [P, HEADS_PER_OCTET, P], F32)) for i in range(2)]
        pv_ps = stack.enter_context(nc.psum_tensor("pv_ps", [P, 512], F32))
        bank = [stack.enter_context(nc.psum_tensor(f"bank{i}", [P, 512], F32)) for i in range(NBANK)]

        w_loaded = sem("w_loaded")
        x_loaded = [sem(f"x_loaded{i}") for i in range(3)]
        ctx_loaded = [sem(f"ctx_loaded{i}") for i in range(2)]
        ffn_w_loaded = sem("ffn_w_loaded")
        small_loaded = sem("small_loaded")
        km_loaded = [sem(f"km_loaded{i}") for i in range(2)]
        stored = sem("stored")
        ident_zeroed = sem("ident_zeroed")
        ident_ready = sem("ident_ready")
        ident16_ready = sem("ident16_ready")
        km_zeroed = sem("km_zeroed")
        v_zeroed = sem("v_zeroed")
        v_ready_ones = sem("v_ready_ones")
        consts_ready = sem("consts_ready")
        tanh_ready = sem("tanh_ready")
        scale_steps = sem("scale_steps")
        w_converted = sem("w_converted")
        w_max_steps = sem("w_max_steps")
        w_max_turned = sem("w_max_turned")
        w_turned = sem("w_turned")
        w_hi_ready = sem("w_hi_ready")
        w_lo_ready = sem("w_lo_ready")
        prep_hi = sem("prep_hi")
        prep_lo = sem("prep_lo")
        filled = [sem(f"filled{i}") for i in range(NBANK)]
        drained = [sem(f"drained{i}") for i in range(NBANK)]
        ctx_turned = sem("ctx_turned")
        stats_ready = sem("stats_ready")
        mean_ready = sem("mean_ready")
        xn_ready = sem("xn_ready")
        stats2_ready = sem("stats2_ready")
        mean2_ready = sem("mean2_ready")
        x1n_ready = sem("x1n_ready")
        root_in_ready = sem("root_in_ready")
        norm_bias_ready = sem("norm_bias_ready")
        root_steps = sem("root_steps")
        xc_hi_ready = sem("xc_hi_ready")
        xc_lo_ready = sem("xc_lo_ready")
        squares_ready = sem("squares_ready")
        sums_ready = sem("sums_ready")
        unit_ready = sem("unit_ready")
        qk_hi_ready = sem("qk_hi_ready")
        qk_lo_ready = sem("qk_lo_ready")
        qk_parts_ready = sem("qk_parts_ready")
        scores_ready = sem("scores_ready")
        probs_ready = sem("probs_ready")
        pv_done = sem("pv_done")
        o_turned_ready = sem("o_turned_ready")
        inv_den_ready = sem("inv_den_ready")
        gated_inv_ready = sem("gated_inv_ready")
        x1_ready = sem("x1_ready")
        x2_hi_ready = sem("x2_hi_ready")
        x2_lo_ready = sem("x2_lo_ready")
        tanh_g_ready = sem("tanh_g_ready")
        silu2_ready = sem("silu2_ready")
        hidden_ready = sem("hidden_ready")
        h_hi_ready = sem("h_hi_ready")
        h_lo_ready = sem("h_lo_ready")
        y_scaled = sem("y_scaled")
        result_ready = sem("result_ready")

        def tile_of(b):
            if isinstance(b, int):
                return x_all[:, b, :]
            return x_all[:, bass.ds(b, 1), :].rearrange("p a d -> p (a d)")

        def dram_tile(t, b):
            if isinstance(b, int):
                return t[b]
            return t[bass.ds(b, 1)].rearrange("a s d -> (a s) d")

        def head_view(n, part):
            per, first, count = ((3, 0, 8), (2, 24, 4))[part]
            return bass.AP(v_blocks, (n * H + first) * BLOCK,
                           [[2 * H * BLOCK, P], [per * BLOCK, count], [BLOCK + SLOTW, per], [1, HD]])

        def run(eng, iteration, first=FIRST):
            for p in range(first, FIRST_STEADY):
                iteration(p)
            if LOOP:
                with eng.Fori(FIRST_STEADY, LAST_STEADY + 1) as p:
                    iteration(p)
            else:
                for p in range(FIRST_STEADY, LAST_STEADY + 1):
                    iteration(p)
            for p in range(LAST_STEADY + 1, PAIRS + 2):
                iteration(p)

        def here(p, task):
            return exists(p, task) if isinstance(p, int) else True

        def has_tile(p, b):
            return 0 <= b < B if isinstance(p, int) else True

        block = stack.enter_context(nc.Block())

        @block.sync
        def _(sp):
            sp.dma_start(w_raw[:, 0, :, :], Wq.rearrange("(c p) d -> p c d", p=P)).then_inc(w_loaded, 16)
            for c, w in enumerate((Wk, Wv)):
                both = w.rearrange("(p two) d -> p two d", two=2)
                sp.dma_start(w_raw[:, 1:3, c, :], both).then_inc(w_loaded, 16)
            sp.dma_start(x_all[:, 0, :], x[0]).then_inc(x_loaded[0], 16)
            sp.dma_start(ctx_sb[:, 0, :], ctx[0]).then_inc(ctx_loaded[0], 16)
            sp.dma_start(x_all[:, 1, :], x[1]).then_inc(x_loaded[1], 16)
            sp.dma_start(ctx_sb[:, 1, :], ctx[1]).then_inc(ctx_loaded[1], 16)
            sp.dma_start(gates[:, 0:1], g_xattn.rearrange("(a d) -> a d", a=1).to_broadcast([P, 1])).then_inc(small_loaded, 16)
            sp.dma_start(gates[:, 1:2], g_ffn.rearrange("(a d) -> a d", a=1).to_broadcast([P, 1])).then_inc(small_loaded, 16)
            sp.dma_start(down_scale[:], s_down.rearrange("(a d) -> a d", a=1).to_broadcast([P, D])).then_inc(small_loaded, 16)
            full = (NJ - 1) * P
            for k, s in enumerate((s_gate, s_up)):
                with nc.allow_non_contiguous_dma(reason="704 scales, one to a partition"):
                    sp.dma_start(scales[:, k, 0:NJ - 1], s[0:full].rearrange("(j p) -> p j", p=P)).then_inc(small_loaded, 16)
                sp.dma_start(scales[0:LAST, k, NJ - 1:NJ], s[full:HID].rearrange("(p j) -> p j", j=1)).then_inc(small_loaded, 16)
            for k, w in enumerate((wq_gate, wq_up)):
                sp.dma_start(gu_int[:, k, 0:NJ - 1, :], w[0:full, :].rearrange("(j p) d -> p j d", p=P)).then_inc(ffn_w_loaded, 16)
                sp.dma_start(gu_int[0:LAST, k, NJ - 1, :], w[full:HID, :]).then_inc(ffn_w_loaded, 16)
            sp.dma_start(dn_int[:], wq_down.rearrange("(c p) h -> p c h", p=P)).then_inc(ffn_w_loaded, 16)
            sp.dma_start(x_all[:, 2:B, :], x[2:B].rearrange("b p d -> p b d")).then_inc(x_loaded[2], 16)

            def iteration(p):
                for e in range(2):
                    b = 2 * p + e
                    if has_tile(p, b + 1):
                        n = 1 - e
                        k, m = use(p, f"stackk{e}")
                        sp.wait_ge(drained[k], m)
                        if not since(b, 1):
                            sp.wait_ge(km_zeroed, 1)
                        for j in range(4):
                            sp.dma_start(k_masked[BLOCK * j:BLOCK * (j + 1), n, j, :, :],
                                         k_stack[BLOCK * j:BLOCK * (j + 1), n, :, :]).then_inc(km_loaded[n], 16)
                    if has_tile(p, b + 2) and has_tile(p, b + 4):
                        sp.wait_ge(ctx_turned, b + 3)
                        sp.dma_start(ctx_sb[:, e, :], dram_tile(ctx, b + 4)).then_inc(ctx_loaded[e], 16)
                    if e == 0 and (not isinstance(p, int) or p >= 2):
                        for k in range(2):
                            done = 2 * (p - 2) + k
                            sp.wait_ge(result_ready, done + 3)
                            sp.dma_start(dram_tile(out, done), tile_of(done)).then_inc(stored, 16)

            for p in range(FIRST, FIRST_STEADY):
                iteration(p)
            if LOOP:
                with sp.Fori(FIRST_STEADY, PAIRS - 2) as p:
                    iteration(p)
            else:
                for p in range(FIRST_STEADY, PAIRS - 2):
                    iteration(p)
            for p in range(PAIRS - 2, PAIRS + 2):
                iteration(p)
            sp.wait_ge(stored, 16 * B)

        @block.gpsimd
        def _(pool):
            nc.gpsimd.memset(ident[:], 0.0).then_inc(ident_zeroed, 1)
            pool.wait_ge(ident_zeroed, 1)
            nc.gpsimd.affine_select(out=ident[:], in_=ident[:], compare_op=ALU.not_equal, fill=1.0, base=0,
                                    pattern=[[-1, P]], channel_multiplier=1).then_inc(ident_ready, 1)
            pool.wait_ge(ident_ready, 1)
            nc.gpsimd.tensor_copy(ident16[:], ident[:]).then_inc(ident16_ready, 1)
            nc.gpsimd.memset(k_masked[:].bitcast(F32), 0.0).then_inc(km_zeroed, 1)
            nc.gpsimd.memset(v_blocks[:], 0.0).then_inc(v_zeroed, 1)
            pool.wait_ge(v_zeroed, 1)
            for e in range(2):
                v = v_blocks[:, e, 0:24 * BLOCK].rearrange("p (t c) -> p t c", c=3 * BLOCK)
                for i in range(3):
                    nc.gpsimd.memset(v[:, :, i * (BLOCK + SLOTW) + HD:i * (BLOCK + SLOTW) + HD + 1], 1.0)
                w = v_blocks[:, e, 24 * BLOCK:].rearrange("p (t c) -> p t c", c=2 * BLOCK)
                for i in range(2):
                    nc.gpsimd.memset(w[:, :, i * (BLOCK + SLOTW) + HD:i * (BLOCK + SLOTW) + HD + 1], 1.0)
                last = nc.gpsimd.memset(w[:, :, 3 * SLOTW - 1:3 * SLOTW], 1.0)
            last.then_inc(v_ready_ones, 1)
            nc.gpsimd.memset(y_sb[:, 0, :], 0.0).then_inc(result_ready, 1)
            nc.gpsimd.memset(y_sb[:, 1, :], 0.0).then_inc(result_ready, 1)

            def split_qk(p, e):
                b = 2 * p + e
                if not has_tile(p, b + 2):
                    return
                pool.wait_ge(qk_hi_ready, b + 3)
                nc.gpsimd.tensor_tensor(qk_parts[:, :, 1, :], qk_unit[:], qk_parts[:, :, 0, :],
                                        ALU.subtract).then_inc(qk_lo_ready, 1)

            def split_hidden(p, q, j):
                n = NJ * (p - q) + j
                pool.wait_ge(h_hi_ready, n + 1)
                r = rows(j)
                nc.gpsimd.tensor_tensor(h_lo[0:r, j, :], hidden[0:r, j % 2, :], h_hi[0:r, j, :].bitcast(F32),
                                        ALU.subtract).then_inc(h_lo_ready, 1)

            def add_attention(p, e):
                b = 2 * p + e - 1
                if has_tile(p, b):
                    k, n = use(p, f"out{e}")
                    pool.wait_ge(drained[k], n)
                    nc.gpsimd.tensor_tensor(tile_of(b), tile_of(b), attn[:], ALU.add).then_inc(x1_ready, 1)

            def add_y(p, e):
                done = 2 * (p - 2) + e
                k, n = use(p, f"y{e}")
                pool.wait_ge(drained[k], n)
                nc.gpsimd.tensor_tensor(y_sb[:, e, :], y_sb[:, e, :], down_scale[:], ALU.mult).then_inc(y_scaled, 1)
                pool.wait_ge(y_scaled, done + 1)
                nc.gpsimd.tensor_tensor(tile_of(done), tile_of(done), y_sb[:, e, :], ALU.add).then_inc(result_ready, 1)

            def real(p, task):
                return here(p, task) and not (isinstance(p, int) and p == 0)

            def iteration(p):
                if real(p, "ffn3"):
                    split_hidden(p, 2, 3)
                    split_hidden(p, 2, 4)
                add_attention(p, 0)
                if real(p, "ffn5"):
                    split_hidden(p, 2, 5)
                split_qk(p, 0)
                if real(p, "y0"):
                    add_y(p, 0)
                    add_y(p, 1)
                add_attention(p, 1)
                if real(p, "ffn0"):
                    split_hidden(p, 1, 0)
                split_qk(p, 1)
                if real(p, "ffn0"):
                    split_hidden(p, 1, 1)
                    split_hidden(p, 1, 2)

            run(pool, iteration)

        @block.scalar
        def _(act):
            for m in range(3):
                act.wait_ge(w_turned, m + 1)
                nc.scalar.copy(w_hi[:, :, m * D:(m + 1) * D],
                               score_ps[m % 2][:, 0:4, :].rearrange("p (k a) n -> p k (a n)", k=KC)
                               ).then_inc(w_hi_ready, 1)
            act.wait_ge(small_loaded, 16 * 7)
            nc.scalar.activation(tanh_gates[:], gates[:], ACT.Tanh).then_inc(tanh_ready, 1)

            def exp_octet(p, e, t):
                b = 2 * p + e
                o = OCTETS * b + t
                if not has_tile(p, b):
                    return
                act.wait_ge(scores_ready, o + 1)
                if since(o, 2):
                    act.wait_ge(pv_done, o - 1)
                nc.scalar.activation(probs[:, t % 2, :], score_ps[t % 2][:].rearrange("p h n -> p (h n)"),
                                     ACT.Exp, scale=float(HD) ** 0.5).then_inc(probs_ready, 1)

            def drain_pv(p, e):
                b = 2 * p + e
                if has_tile(p, b - 1):
                    act.wait_ge(pv_done, OCTETS * b)
                    nc.scalar.copy(o_turned[:, 1 - e, :], pv_ps[:, 0:3 * P]).then_inc(o_turned_ready, 1)

            def drain_v(p, e):
                b = 2 * p + e
                if not has_tile(p, b + 1):
                    return
                n = 1 - e
                k, m = use(p, f"v{e}")
                act.wait_ge(filled[k], m)
                if not since(b, 0):
                    act.wait_ge(v_ready_ones, 1)
                src = bank[k][:, 0:24 * HD].rearrange("p (t i d) -> p t i d", i=3, d=HD)
                nc.scalar.copy(head_view(n, 0), src)
                src = bank[k][:, 24 * HD:D].rearrange("p (t i d) -> p t i d", i=2, d=HD)
                nc.scalar.copy(head_view(n, 1), src).then_inc(drained[k], 1)

            def turn_hi(p, e):
                b = 2 * p + e
                if has_tile(p, b + 2):
                    k, m = use(p, f"turn{e}")
                    act.wait_ge(filled[k], m)
                    nc.scalar.copy(xc_hi[:, e, :, :].rearrange("p a n -> p (a n)"), bank[k][:]).then_inc(xc_hi_ready, 1)

            def stack_keys(p, e):
                b = 2 * p + e
                if has_tile(p, b + 1):
                    k, m = use(p, f"stackk{e}")
                    act.wait_ge(filled[k], m)
                    nc.scalar.copy(k_stack[:, 1 - e, :, :].rearrange("p g n -> p (g n)"),
                                   bank[k][:].bitcast(F16)).then_inc(drained[k], 1)

            def square(p, e):
                b = 2 * p + e
                if has_tile(p, b + 2):
                    k, m = use(p, f"qk{e}")
                    act.wait_ge(filled[k], m)
                    if since(b, -1):
                        act.wait_ge(sums_ready, b + 2)
                    nc.scalar.activation(squares[:], bank[k][:], ACT.Square).then_inc(squares_ready, 1)
                    if since(b, -1):
                        act.wait_ge(unit_ready, b + 2)
                    nc.scalar.copy(qk_raw[:].rearrange("p h d -> p (h d)"), bank[k][:]).then_inc(drained[k], 1)

            def normalize(p, e):
                b = 2 * p + e + 3
                if has_tile(p, b):
                    act.wait_ge(norm_bias_ready, b + 1)
                    nc.scalar.activation(xn[:, 1 - e, :], tile_of(b), ACT.Identity, bias=norm_bias[:, 0:1],
                                         scale=root_y[:, 2 * H:2 * H + 1]).then_inc(xn_ready, 1)

            def normalize2(p, e):
                b = 2 * p + e - 1
                if has_tile(p, b):
                    act.wait_ge(norm_bias_ready, b + 5)
                    nc.scalar.activation(x1n[:, 1 - e, :], tile_of(b), ACT.Identity, bias=norm_bias[:, 1:2],
                                         scale=root_y[:, 2 * H + 1:2 * H + 2]).then_inc(x1n_ready, 1)

            def drain_y(p, e):
                task = f"y{e}"
                if not here(p, task):
                    return
                k, m = use(p, task)
                if isinstance(p, int) and p == 0:
                    prep(task, k, m)
                    return
                done = 2 * (p - 2) + e
                act.wait_ge(filled[k], m)
                act.wait_ge(result_ready, done + 1)
                nc.scalar.copy(y_sb[:, e, :], bank[k][:, 0:D]).then_inc(drained[k], 1)

            def tanh_chunk(p, q, j):
                task = f"ffn{j}"
                if not here(p, task):
                    return
                k, m = use(p, task)
                if isinstance(p, int) and p == 0:
                    prep(task, k, m)
                    return
                n = NJ * (p - q) + j
                act.wait_ge(filled[k], m)
                if since(n, 2):
                    act.wait_ge(silu2_ready, n - 1)
                r = rows(j)
                nc.scalar.activation(tanh_g[0:r, j % 2, :], bank[k][0:r, 0:TOK], ACT.Tanh,
                                     scale=half_gate[0:r, j:j + 1]).then_inc(tanh_g_ready, 1)

            def prep(task, k, m):
                part = PREP[task]
                act.wait_ge(filled[k], m)
                if part < NJ:
                    nc.scalar.copy(gu_hi[:, part, :, :, 0:rows(part)],
                                   bank[k][:].rearrange("p (a c n) -> p a c n", a=2, c=KC)[:, :, :, 0:rows(part)]
                                   ).then_inc(prep_hi, 1)
                    return
                for a in range(2):
                    j = 2 * (part - NJ) + a
                    last = nc.scalar.copy(dn_hi[0:rows(j), j, :], bank[k][0:rows(j), a * D:(a + 1) * D])
                last.then_inc(prep_hi, 1)

            def turn2_hi(p):
                if not here(p, "turn2"):
                    return
                k, m = use(p, "turn2")
                if isinstance(p, int) and p == 0:
                    prep("turn2", k, m)
                    return
                act.wait_ge(filled[k], m)
                nc.scalar.copy(x2_hi[:].rearrange("p c n -> p (c n)"), bank[k][:]).then_inc(x2_hi_ready, 1)

            def iteration(p):
                first = isinstance(p, int) and p == 0
                if first:
                    act.wait_ge(scale_steps, 2)
                exp_octet(p, 0, 0)
                drain_pv(p, 0)
                turn_hi(p, 0)
                tanh_chunk(p, 2, 3)
                tanh_chunk(p, 2, 4)
                exp_octet(p, 0, 1)
                stack_keys(p, 0)
                square(p, 0)
                exp_octet(p, 0, 2)
                drain_v(p, 0)
                tanh_chunk(p, 2, 5)
                exp_octet(p, 0, 3)
                normalize2(p, 0)
                normalize(p, 0)
                drain_y(p, 0)
                exp_octet(p, 1, 0)
                drain_pv(p, 1)
                turn_hi(p, 1)
                turn2_hi(p)
                drain_y(p, 1)
                exp_octet(p, 1, 1)
                stack_keys(p, 1)
                square(p, 1)
                exp_octet(p, 1, 2)
                drain_v(p, 1)
                tanh_chunk(p, 1, 0)
                exp_octet(p, 1, 3)
                normalize2(p, 1)
                normalize(p, 1)
                tanh_chunk(p, 1, 1)
                tanh_chunk(p, 1, 2)

            run(act, iteration)

        @block.vector
        def _(dve):
            nc.vector.memset(mean_var[:], 1.0)
            nc.vector.memset(root_in[:], 1.0)
            nc.vector.memset(weight_max[:], 0.0)
            for m in range(3):
                dve.wait_ge(w_hi_ready, m + 1)
                nc.vector.tensor_tensor(w_lo[:, :, m * D:(m + 1) * D],
                                        score_ps[m % 2][:, 0:4, :].rearrange("p (k a) n -> p k (a n)", k=KC),
                                        w_hi[:, :, m * D:(m + 1) * D].bitcast(F32), ALU.subtract).then_inc(w_lo_ready, 1)

            def statistics(p, e):
                b = 2 * p + e + 3
                if not has_tile(p, b):
                    return
                if isinstance(b, int) and b <= 2:
                    dve.wait_ge(x_loaded[b], 16)
                nc.vector.bn_stats(stats[:, 0, :], tile_of(b)).then_inc(stats_ready, 1)

            def mean(p, e):
                b = 2 * p + e + 3
                if has_tile(p, b):
                    if not has_tile(p, b - 2):
                        dve.wait_ge(stats_ready, b + 1)
                    nc.vector.bn_aggr(mean_var[:, 0, :], stats[:, 0, :]).then_inc(mean_ready, 1)

            def has_roots(p, b):
                return -3 <= b <= B if isinstance(p, int) else True

            def root_inputs(p, e):
                b = 2 * p + e
                if not has_roots(p, b):
                    return
                if has_tile(p, b - 1):
                    dve.wait_ge(stats2_ready, b)
                if has_tile(p, b + 2):
                    dve.wait_ge(sums_ready, b + 3)
                    nc.vector.tensor_scalar(root_in[:, 0:2 * H], sums[:], HD * RMS_EPS, None, ALU.add)
                if has_tile(p, b - 1):
                    nc.vector.bn_aggr(mean_var[:, 1, :], stats[:, 1, :]).then_inc(mean2_ready, 1)
                    dve.wait_ge(mean2_ready, b)
                if has_tile(p, b + 3):
                    dve.wait_ge(mean_ready, b + 4)
                nc.vector.tensor_scalar(root_in[:, 2 * H:], mean_var[:, :, 1], LN_EPS, None,
                                        ALU.add).then_inc(root_in_ready, 1)

            def root(p, e, first, last):
                b = 2 * p + e
                if not has_roots(p, b):
                    return
                for step in range(first, last):
                    if step == 0:
                        dve.wait_ge(root_in_ready, b + 4)
                        if since(b, -2):
                            dve.wait_ge(xn_ready, min(b + 3, B) if isinstance(b, int) else b + 3)
                        if since(b, 2):
                            dve.wait_ge(x1n_ready, b - 1)
                        bits = nc.vector.tensor_scalar(root_y[:].bitcast(I32), root_in[:].bitcast(I32), -0.5, START_BITS, ALU.mult, ALU.add)
                        bits.then_inc(root_steps, 1)
                        continue
                    dve.wait_ge(root_steps, RSQRT_STEPS * (b + 3) + step)
                    scale = START_SCALE if step <= 4 else MID_SCALE
                    k = (step - 1) % 4
                    if k == 0:
                        ins = nc.vector.tensor_tensor(root_xy[:], root_in[:], root_y[:], ALU.mult)
                    elif k == 1:
                        ins = nc.vector.tensor_tensor(root_v[:], root_xy[:], root_y[:], ALU.mult)
                    elif k == 2:
                        ins = nc.vector.scalar_tensor_tensor(out=root_p[:], in0=root_v[:], scalar=-10 / 3 * scale ** 2,
                                                             in1=root_v[:], op0=ALU.add, op1=ALU.mult)
                    else:
                        ins = nc.vector.scalar_tensor_tensor(out=root_y[:], in0=root_p[:], scalar=5 * scale ** 4,
                                                             in1=root_y[:], op0=ALU.add, op1=ALU.mult)
                    ins.then_inc(root_steps, 1)

            def bias(p, e):
                b = 2 * p + e
                if has_roots(p, b):
                    dve.wait_ge(root_steps, RSQRT_STEPS * (b + 4))
                    nc.vector.scalar_tensor_tensor(out=norm_bias[:], in0=mean_var[:, :, 0], scalar=-1.0, in1=root_y[:, 2 * H:],
                                                   op0=ALU.mult, op1=ALU.mult).then_inc(norm_bias_ready, 1)

            def turn_lo(p, e):
                b = 2 * p + e
                if has_tile(p, b + 2):
                    k, m = use(p, f"turn{e}")
                    dve.wait_ge(filled[k], m)
                    dve.wait_ge(xc_hi_ready, b + 3)
                    nc.vector.tensor_tensor(xc_lo[:, e, :, :].rearrange("p a n -> p (a n)"), bank[k][:],
                                            xc_hi[:, e, :, :].rearrange("p a n -> p (a n)").bitcast(F32),
                                            ALU.subtract).then_inc(drained[k], 1)

            def sum_squares(p, e):
                b = 2 * p + e
                if has_tile(p, b + 2):
                    dve.wait_ge(squares_ready, b + 3)
                    nc.vector.tensor_reduce(sums[:], squares[:].rearrange("p (h d) -> p h d", d=HD), AX.X,
                                            ALU.add).then_inc(sums_ready, 1)

            def qk_norm(p, e):
                b = 2 * p + e
                if not has_tile(p, b + 2):
                    return
                dve.wait_ge(root_steps, RSQRT_STEPS * (b + 4))
                k, m = use(p, f"qk{e}")
                dve.wait_ge(drained[k], m)
                if since(b, -1):
                    dve.wait_ge(qk_lo_ready, b + 2)
                nc.vector.tensor_tensor(qk_unit[:], qk_raw[:],
                                        root_y[:, 0:2 * H].unsqueeze(2).to_broadcast([P, 2 * H, HD]),
                                        ALU.mult).then_inc(unit_ready, 1)

            def qk_upper(p, e):
                b = 2 * p + e
                if not has_tile(p, b + 2):
                    return
                dve.wait_ge(unit_ready, b + 3)
                if since(b, -1):
                    k, m = use(p, f"stackk{e}")
                    dve.wait_ge(filled[k], m)
                nc.vector.tensor_copy(qk_parts[:, :, 0, :], qk_unit[:]).then_inc(qk_hi_ready, 1)

            def qk_double(p, e):
                b = 2 * p + e
                if not has_tile(p, b + 1):
                    return
                dve.wait_ge(qk_lo_ready, b + 2)
                if has_tile(p, b + 3):
                    dve.wait_ge(stats_ready, b + 4)
                words = qk_parts[:].rearrange("p h a d -> p h (a d)").bitcast(F32)
                W = HD // 2
                nc.vector.tensor_copy(words[:, 0:H, 2 * W:4 * W], words[:, 0:H, 0:2 * W])
                nc.vector.tensor_copy(words[:, H:2 * H, 2 * W:3 * W], words[:, H:2 * H, W:2 * W])
                nc.vector.tensor_copy(words[:, H:2 * H, 3 * W:4 * W], words[:, H:2 * H, 0:W]).then_inc(qk_parts_ready, 1)

            def stack_queries(p, e):
                b = 2 * p + e
                if has_tile(p, b + 1):
                    k, m = use(p, f"stackq{e}")
                    dve.wait_ge(filled[k], m)
                    nc.vector.tensor_copy(q_stack[:, 1 - e, :, :].rearrange("p g n -> p (g n)"),
                                          bank[k][:].bitcast(F16)).then_inc(drained[k], 1)

            def out_reciprocal(p, e):
                b = 2 * p + e - 1
                if has_tile(p, b):
                    k, m = use(p, f"out{e}")
                    dve.wait_ge(filled[k], m)
                    nc.vector.reciprocal(inv_den[:], out_slots(k)[:, :, :, HD]).then_inc(inv_den_ready, 1)

            def out_slots(k):
                blocks = bank[k][:, 0:3 * P].rearrange("p (t c) -> p t c", c=BLOCK)
                return blocks[:, :, 0:3 * SLOTW].rearrange("p t (i c) -> p t i c", c=SLOTW)

            def gate_reciprocal(p, e):
                b = 2 * p + e - 1
                if has_tile(p, b):
                    dve.wait_ge(inv_den_ready, b + 1)
                    nc.vector.tensor_scalar(gated_inv[:], inv_den[:], tanh_gates[:, 0:1], None,
                                            ALU.mult).then_inc(gated_inv_ready, 1)

            def out_divide(p, e):
                b = 2 * p + e - 1
                if not has_tile(p, b):
                    return
                k, m = use(p, f"out{e}")
                dve.wait_ge(gated_inv_ready, b + 1)
                if since(b, 1):
                    dve.wait_ge(x1_ready, b)
                for t0, t1, per, h0 in ((0, 8, 3, 0), (8, 12, 2, 24)):
                    dst = attn[:, h0 * HD:(h0 + (t1 - t0) * per) * HD].rearrange("p (t i d) -> p t i d", i=per, d=HD)
                    last = nc.vector.tensor_tensor(dst, out_slots(k)[:, t0:t1, 0:per, 0:HD],
                                                   gated_inv[:, t0:t1, 0:per].unsqueeze(3).to_broadcast([P, t1 - t0, per, HD]),
                                                   ALU.mult)
                last.then_inc(drained[k], 1)

            def statistics2(p, e):
                b = 2 * p + e - 1
                if has_tile(p, b):
                    dve.wait_ge(x1_ready, b + 1)
                    nc.vector.bn_stats(stats[:, 1, :], tile_of(b)).then_inc(stats2_ready, 1)

            def gate(p, q, j):
                task = f"ffn{j}"
                if not here(p, task):
                    return
                k, m = use(p, task)
                if isinstance(p, int) and p == 0:
                    prep(task, k, m)
                    return
                n = NJ * (p - q) + j
                r = rows(j)
                if isinstance(n, int) and n == 0:
                    dve.wait_ge(scale_steps, 5)
                dve.wait_ge(tanh_g_ready, n + 1)
                nc.vector.scalar_tensor_tensor(out=silu2[0:r, j % 2, :], in0=tanh_g[0:r, j % 2, :], scalar=1.0,
                                               in1=bank[k][0:r, 0:TOK], op0=ALU.add, op1=ALU.mult).then_inc(silu2_ready, 1)

            def up(p, q, j):
                task = f"ffn{j}"
                if not here(p, task) or isinstance(p, int) and p == 0:
                    return
                k, m = use(p, task)
                n = NJ * (p - q) + j
                r = rows(j)
                dve.wait_ge(silu2_ready, n + 1)
                if since(n, 2):
                    dve.wait_ge(h_lo_ready, n - 1)
                nc.vector.scalar_tensor_tensor(out=hidden[0:r, j % 2, :], in0=silu2[0:r, j % 2, :], scalar=scales[0:r, 2, j:j + 1],
                                               in1=bank[k][0:r, TOK:2 * TOK], op0=ALU.mult, op1=ALU.mult).then_inc(drained[k], 1)

            def upper(p, q, j):
                task = f"ffn{j}"
                if not here(p, task) or isinstance(p, int) and p == 0:
                    return
                k, m = use(p, task)
                r = rows(j)
                dve.wait_ge(drained[k], m)
                nc.vector.tensor_copy(h_hi[0:r, j, :], hidden[0:r, j % 2, :]).then_inc(h_hi_ready, 1)

            def prep(task, k, m):
                part = PREP[task]
                dve.wait_ge(filled[k], m)
                dve.wait_ge(prep_hi, part + 1)
                if part < NJ:
                    r = rows(part)
                    nc.vector.tensor_tensor(gu_lo[:, part, :, :, 0:r],
                                            bank[k][:].rearrange("p (a c n) -> p a c n", a=2, c=KC)[:, :, :, 0:r],
                                            gu_hi[:, part, :, :, 0:r].bitcast(F32), ALU.subtract).then_inc(drained[k], 1)
                    return
                for a in range(2):
                    j = 2 * (part - NJ) + a
                    last = nc.vector.tensor_tensor(dn_lo[0:rows(j), j, :], bank[k][0:rows(j), a * D:(a + 1) * D],
                                                   dn_hi[0:rows(j), j, :].bitcast(F32), ALU.subtract)
                last.then_inc(drained[k], 1)

            def turn2_lo(p):
                if not here(p, "turn2"):
                    return
                k, m = use(p, "turn2")
                if isinstance(p, int) and p == 0:
                    prep("turn2", k, m)
                    return
                dve.wait_ge(filled[k], m)
                dve.wait_ge(x2_hi_ready, p)
                nc.vector.tensor_tensor(x2_lo[:].rearrange("p c n -> p (c n)"), bank[k][:],
                                        x2_hi[:].rearrange("p c n -> p (c n)").bitcast(F32),
                                        ALU.subtract).then_inc(drained[k], 1)

            def prep_y(p, e):
                if isinstance(p, int) and p == 0:
                    prep(f"y{e}", *use(p, f"y{e}"))

            def scale_setup():
                dve.wait_ge(small_loaded, 16 * 7)
                for r, j0, j1 in ((P, 0, NJ - 1), (LAST, NJ - 1, NJ)):
                    nc.vector.tensor_scalar(half_gate[0:r, j0:j1], scales[0:r, 0, j0:j1], 0.5, None, ALU.mult).then_inc(scale_steps, 1)
                dve.wait_ge(scale_steps, 2)
                for r, j0, j1 in ((P, 0, NJ - 1), (LAST, NJ - 1, NJ)):
                    nc.vector.tensor_tensor(scales[0:r, 2, j0:j1], half_gate[0:r, j0:j1], scales[0:r, 1, j0:j1],
                                            ALU.mult).then_inc(scale_steps, 1)
                dve.wait_ge(tanh_ready, 1)
                nc.vector.tensor_scalar(down_scale[:], down_scale[:], tanh_gates[:, 1:2], None, ALU.mult).then_inc(scale_steps, 1)

            def convert_weights():
                dve.wait_ge(ffn_w_loaded, 16 * 5)
                for k in range(2):
                    nc.vector.tensor_scalar(gu_raw[:, k, 0:NJ - 1, :], gu_int[:, k, 0:NJ - 1, :], -ZERO_POINT, None, ALU.add)
                    nc.vector.tensor_scalar(gu_raw[0:LAST, k, NJ - 1, :], gu_int[0:LAST, k, NJ - 1, :], -ZERO_POINT, None, ALU.add)
                nc.vector.tensor_scalar(dn_raw[:], dn_int[:], -ZERO_POINT, None, ALU.add).then_inc(w_converted, 1)

            def widest_weight():
                dve.wait_ge(w_converted, 1)
                nc.vector.tensor_reduce(weight_max[:, 0:1], gu_raw[:, :, 0:NJ - 1, :], AX.XYZ, ALU.max, apply_absolute_value=True)
                nc.vector.tensor_reduce(weight_max[0:LAST, 1:2], gu_raw[0:LAST, :, NJ - 1, :], AX.XY, ALU.max, apply_absolute_value=True)
                nc.vector.tensor_reduce(weight_max[:, 2:3], dn_raw[:], AX.XY, ALU.max, apply_absolute_value=True).then_inc(w_max_steps, 1)
                dve.wait_ge(w_max_steps, 1)
                nc.vector.tensor_reduce(weight_max[:, 3:4], weight_max[:, 0:3], AX.X, ALU.max).then_inc(w_max_steps, 1)
                dve.wait_ge(w_max_turned, 1)
                nc.vector.tensor_reduce(wide_max[:], pv_ps[0:1, 0:P], AX.X, ALU.max).then_inc(w_max_steps, 1)
                dve.wait_ge(w_max_steps, 3)
                nc.vector.tensor_scalar(wide[:], wide_max[:], F32R_INTEGERS, None, ALU.is_gt).then_inc(w_max_steps, 1)

            def roots(p, e, q, j):
                root_inputs(p, e)
                root(p, e, 0, 1)
                gate(p, q, j)
                root(p, e, 1, 2)
                up(p, q, j)
                root(p, e, 2, 3)
                upper(p, q, j)
                root(p, e, 3, 9)
                bias(p, e)
                qk_norm(p, e)
                qk_upper(p, e)

            def iteration(p):
                turn_lo(p, 0)
                statistics(p, 0)
                qk_double(p, 0)
                mean(p, 0)
                gate(p, 2, 3)
                up(p, 2, 3)
                gate(p, 2, 4)
                upper(p, 2, 3)
                up(p, 2, 4)
                out_reciprocal(p, 0)
                upper(p, 2, 4)
                gate_reciprocal(p, 0)
                out_divide(p, 0)
                stack_queries(p, 0)
                sum_squares(p, 0)
                statistics2(p, 0)
                roots(p, 0, 2, 5)
                prep_y(p, 0)
                turn_lo(p, 1)
                statistics(p, 1)
                qk_double(p, 1)
                mean(p, 1)
                turn2_lo(p)
                prep_y(p, 1)
                out_reciprocal(p, 1)
                gate_reciprocal(p, 1)
                out_divide(p, 1)
                stack_queries(p, 1)
                sum_squares(p, 1)
                statistics2(p, 1)
                roots(p, 1, 1, 0)
                gate(p, 1, 1)
                up(p, 1, 1)
                gate(p, 1, 2)
                upper(p, 1, 1)
                up(p, 1, 2)
                upper(p, 1, 2)
                if isinstance(p, int) and p == -1:
                    scale_setup()
                    convert_weights()
                    widest_weight()

            run(dve, iteration)

        @block.tensor
        def _(pe):
            pe.wait_ge(ident_ready, 1)
            pe.wait_ge(w_loaded, 16 * 3)
            for m in range(3):
                if m == 2:
                    pe.wait_ge(w_lo_ready, 1)
                for k in range(KC):
                    for c in range(KC):
                        last = nc.tensor.transpose(score_ps[m % 2][:, KC * k + c, :], w_raw[:, m, c, k * P:(k + 1) * P], ident[:])
                last.then_inc(w_turned, 1)

            def claim(p, task):
                k, m = use(p, task)
                if since(m, 2):
                    pe.wait_ge(drained[k], m - 1)
                return k

            def scores(p, e, t):
                b = 2 * p + e
                if not has_tile(p, b):
                    return
                o = OCTETS * b + t
                if t == 0:
                    k, m = use(p, "stackq0") if e else use(p - 1, "stackq1")
                    pe.wait_ge(drained[k], m)
                    pe.wait_ge(km_loaded[e], 64 * (p + 1))
                if isinstance(o, int) and o == 0:
                    pe.wait_ge(w_lo_ready, 3)
                if since(o, 2):
                    pe.wait_ge(probs_ready, o - 1)
                for s in range(HEADS_PER_OCTET):
                    h = place(HEADS_PER_OCTET * t + s)[0]
                    last = nc.tensor.matmul(score_ps[t % 2][:, s, :], k_masked[:, e, h % 4, h // 4, :],
                                            q_stack[:, e, h // 4, :], start=True, stop=True)
                last.then_inc(scores_ready, 1)

            def weigh(p, e, t):
                b = 2 * p + e
                o = OCTETS * b + t - 1
                e, t = (e, t - 1) if t else (1 - e, OCTETS - 1)
                b = b if t < OCTETS - 1 else b - 1
                if not has_tile(p, b):
                    return
                pe.wait_ge(probs_ready, o + 1)
                if t == 0:
                    pe.wait_ge(v_ready_of(p, b, e)[0], v_ready_of(p, b, e)[1])
                    if since(b, 1):
                        pe.wait_ge(o_turned_ready, b)
                    else:
                        pe.wait_ge(w_max_steps, 3)
                for s in range(HEADS_PER_OCTET):
                    h, region, quadrant, i = place(HEADS_PER_OCTET * t + s)
                    last = nc.tensor.matmul(pv_ps[BLOCK * quadrant:BLOCK * (quadrant + 1), region * P:(region + 1) * P],
                                            v_blocks[:, e, h * BLOCK:(h + 1) * BLOCK],
                                            probs[:, t % 2, s * P:(s + 1) * P],
                                            start=(i == 0), stop=(i == (2 if region < 2 else 1)),
                                            tile_position=(0, BLOCK * quadrant))
                last.then_inc(pv_done, 1)

            def v_ready_of(p, b, e):
                if e == 0:
                    k, m = use(p - 1, "v1")
                    return drained[k], m
                k, m = use(p, "v0")
                return drained[k], m

            def turn(p, e):
                b = 2 * p + e
                if not has_tile(p, b + 2):
                    return
                k = claim(p, f"turn{e}")
                pe.wait_ge(ctx_loaded[e], 16 * (p + 2))
                for c in range(KC):
                    last = nc.tensor.transpose(bank[k][:, (KC + c) * P:(KC + c + 1) * P], ctx_sb[:, e, c * P:(c + 1) * P], ident[:])
                last.then_inc(ctx_turned, 1)
                pe.wait_ge(xn_ready, b + 3)
                for c in range(KC):
                    last = nc.tensor.transpose(bank[k][:, c * P:(c + 1) * P], xn[:, e, c * P:(c + 1) * P], ident[:])
                last.then_inc(filled[k], 1)

            def project(dst, tile, source, column):
                n = 0
                for c in range(KC):
                    for a, w in ((xc_hi, w_hi), (xc_hi, w_lo), (xc_lo, w_hi)):
                        n += 1
                        last = nc.tensor.matmul(dst, a[:, tile, KC * source + c, :], w[:, c, column * D:(column + 1) * D],
                                                start=(n == 1), stop=(n == 3 * KC))
                return last

            def queries_keys(p, e):
                b = 2 * p + e
                if not has_tile(p, b + 2):
                    return
                k = claim(p, f"qk{e}")
                j, m = use(p, f"turn{e}")
                pe.wait_ge(drained[j], m)
                if isinstance(b, int) and b == -2:
                    pe.wait_ge(w_lo_ready, 3)
                project(bank[k][:, 0:D], e, 0, 0)
                project(bank[k][:, D:2 * D], e, 1, 1).then_inc(filled[k], 1)

            def values(p, e):
                b = 2 * p + e
                if not has_tile(p, b + 1):
                    return
                k = claim(p, f"v{e}")
                project(bank[k][:, 0:D], 1 - e, 1, 2).then_inc(filled[k], 1)

            def stacks(p, e):
                b = 2 * p + e
                if not has_tile(p, b + 1):
                    return
                if isinstance(b, int) and b == -1:
                    pe.wait_ge(ident16_ready, 1)
                for name in ("stackq", "stackk"):
                    k = claim(p, f"{name}{e}")
                    if name == "stackq":
                        pe.wait_ge(qk_parts_ready, b + 2)
                    dst = bank[k][:].bitcast(F16)
                    for g in range(GROUPS):
                        h = 4 * g + (0 if name == "stackq" else H)
                        src = qk_parts[:, h:h + 4, :, :].rearrange("p h a d -> p (h a d)")
                        last = nc.tensor.transpose(dst[:, g * P:(g + 1) * P], src, ident16[:])
                    last.then_inc(filled[k], 1)

            def out_rows(p, e):
                b = 2 * p + e
                if not has_tile(p, b - 1):
                    return
                k = claim(p, f"out{e}")
                pe.wait_ge(o_turned_ready, b)
                for r in range(3):
                    last = nc.tensor.transpose(bank[k][:, r * P:(r + 1) * P], o_turned[:, 1 - e, r * P:(r + 1) * P], ident[:])
                last.then_inc(filled[k], 1)

            def prep(task):
                part = PREP[task]
                k = claim(0, task)
                pe.wait_ge(w_converted, 1)
                if part < NJ:
                    r = rows(part)
                    for a in range(2):
                        for c in range(KC):
                            col = (KC * a + c) * P
                            last = nc.tensor.transpose(bank[k][:, col:col + r], gu_raw[0:r, a, part, c * P:(c + 1) * P], ident[0:r, 0:r])
                else:
                    for a in range(2):
                        j = 2 * (part - NJ) + a
                        for c in range(KC):
                            col = a * D + c * P
                            last = nc.tensor.transpose(bank[k][0:rows(j), col:col + P], dn_raw[:, c, j * P:j * P + rows(j)], ident[:])
                last.then_inc(filled[k], 1)

            def turn2(p):
                if not here(p, "turn2"):
                    return
                if isinstance(p, int) and p == 0:
                    return prep("turn2")
                k = claim(p, "turn2")
                pe.wait_ge(x1n_ready, 2 * p)
                for c in range(KC):
                    for e in range(2):
                        last = nc.tensor.transpose(bank[k][:, c * TOK + e * P:c * TOK + (e + 1) * P], x1n[:, e, c * P:(c + 1) * P], ident[:])
                last.then_inc(filled[k], 1)

            def chunk(p, j, wide_weights):
                task = f"ffn{j}"
                if not here(p, task):
                    return
                if isinstance(p, int) and p == 0:
                    return prep(task)
                k = claim(p, task)
                if j == 0:
                    i, m = use(p, "turn2")
                    pe.wait_ge(drained[i], m)
                r = rows(j)
                for a in range(2):
                    n = 0
                    for c in range(KC):
                        for w, xx in products(wide_weights, gu_hi, gu_lo, x2_hi, x2_lo):
                            n += 1
                            last = nc.tensor.matmul(bank[k][0:r, a * TOK:(a + 1) * TOK], w[:, j, a, c, 0:r], xx[:, c, :],
                                                    start=(n == 1), stop=(n == (4 if wide_weights else 2) * KC))
                last.then_inc(filled[k], 1)

            def products(wide_weights, w_upper, w_lower, upper, lower):
                pairs = [(w_upper, upper), (w_upper, lower)]
                return pairs + [(w_lower, upper), (w_lower, lower)] if wide_weights else pairs

            def down(p, e, wide_weights):
                task = f"y{e}"
                if not here(p, task):
                    return
                if isinstance(p, int) and p == 0:
                    return prep(task)
                k = claim(p, task)
                n = 0
                for j in range(NJ):
                    if e == 0 and j >= 3:
                        pe.wait_ge(h_lo_ready, NJ * (p - 2) + j + 1)
                    r = rows(j)
                    for w, hh in products(wide_weights, dn_hi, dn_lo, h_hi, h_lo):
                        n += 1
                        last = nc.tensor.matmul(bank[k][:, 0:D], hh[0:r, j, e * P:(e + 1) * P], w[0:r, j, :],
                                                start=(n == 1), stop=(n == (4 if wide_weights else 2) * NJ))
                last.then_inc(filled[k], 1)

            def iteration(p, wide_weights=False):
                scores(p, 0, 0)
                weigh(p, 0, 0)
                turn(p, 0)
                chunk(p, 3, wide_weights)
                chunk(p, 4, wide_weights)

                scores(p, 0, 1)
                out_rows(p, 0)
                weigh(p, 0, 1)
                stacks(p, 0)
                queries_keys(p, 0)

                scores(p, 0, 2)
                weigh(p, 0, 2)
                values(p, 0)
                chunk(p, 5, wide_weights)

                scores(p, 0, 3)
                weigh(p, 0, 3)
                down(p, 0, wide_weights)

                scores(p, 1, 0)
                weigh(p, 1, 0)
                turn(p, 1)
                turn2(p)
                down(p, 1, wide_weights)

                scores(p, 1, 1)
                out_rows(p, 1)
                weigh(p, 1, 1)
                stacks(p, 1)
                queries_keys(p, 1)

                scores(p, 1, 2)
                weigh(p, 1, 2)
                values(p, 1)
                chunk(p, 0, wide_weights)

                scores(p, 1, 3)
                weigh(p, 1, 3)
                chunk(p, 1, wide_weights)
                chunk(p, 2, wide_weights)

            for p in range(FIRST, 1):
                iteration(p)
                if p == -1:
                    pe.wait_ge(w_max_steps, 2)
                    nc.tensor.transpose(pv_ps[0:1, 0:P], weight_max[:, 3:4], ident[:]).then_inc(w_max_turned, 1)
            pe.wait_ge(w_max_steps, 4)
            any_wide = pe.alloc_register("any_wide")
            pe.reg_load(any_wide, wide[:])
            with pe.If_ne(any_wide, 0):
                run(pe, lambda p: iteration(p, True), 1)
            with pe.Else():
                run(pe, lambda p: iteration(p, False), 1)


INPUTS = ["x", "ctx_2048", "g_xattn", "g_ffn", "L0_xattn_Wq", "L0_xattn_Wk", "L0_xattn_Wv", "L0_ffn_wq_gate",
          "L0_ffn_s_gate", "L0_ffn_wq_up", "L0_ffn_s_up", "L0_ffn_wq_down", "L0_ffn_s_down"]


def kernel(**inputs):
    import numpy as np
    import concourse.bacc as bacc
    from concourse.bass_utils import run_bass_kernel_spmd

    nc = bacc.Bacc("TRN2", target_bir_lowering=False, num_devices=1)
    arrays, args = {}, []
    for name in INPUTS:
        a = np.ascontiguousarray(inputs[name])
        arrays[f"{name}_dram"] = a
        args.append(nc.dram_tensor(f"{name}_dram", a.shape, mybir.dt.from_np(a.dtype), kind="ExternalInput").ap())
    x = arrays["x_dram"]
    args.append(nc.dram_tensor("out_dram", x.shape, mybir.dt.from_np(x.dtype), kind="ExternalOutput").ap())
    build_program(nc, *args)
    result = run_bass_kernel_spmd(nc, [arrays], core_ids=[0])
    return result.results[0]["out_dram"]
```

```python
from contextlib import ExitStack

import concourse.bass as bass
from concourse import mybir

ALU = mybir.AluOpType
ACT = mybir.ActivationFunctionType
AX = mybir.AxisListType
F32 = mybir.dt.float32
F32R = mybir.dt.float32r
F16 = mybir.dt.float16
I32 = mybir.dt.int32

P = 128
HD = 8
LN_EPS = 1e-5
RMS_EPS = 1e-6
ZERO_POINT = 128.0

MID_SCALE = 0.375 ** 0.2
NEWTON_EXCESS = 0.001
START_SCALE = (0.5 * MID_SCALE / (1 - NEWTON_EXCESS)) ** (1 / 3)
START_BITS = 1593900416.0
ROOT_STEPS = 7
UNIT = 64.0
F32R_INTEGERS = 4096.0
BLOCK = 32
SLOTW = HD + 1
HEADS_PER_OCTET = 8


def build_program(nc, x, ctx, g_xattn, g_ffn, Wq, Wk, Wv, wq_gate, s_gate, wq_up, s_up, wq_down, s_down, out):
    B, S, D = x.shape
    HID = wq_gate.shape[0]
    H = D // HD
    KC = D // P
    NJ = -(-HID // P)
    LAST = HID - (NJ - 1) * P
    PAIRS = B // 2
    OCTETS = H // HEADS_PER_OCTET
    GROUPS = H // 4
    TOK = 2 * S
    assert S == P and D == 2 * P and H == 32 and B % 2 == 0 and NJ == 6

    def rows(j):
        return P if j < NJ - 1 else LAST

    def place(n):
        region, i, quadrant = (n // 12, n % 12 // 4, n % 4) if n < 24 else (2, (n - 24) // 4, n % 4)
        head = 12 * region + 3 * quadrant + i if region < 2 else 24 + 2 * quadrant + i
        return head, region, quadrant, i

    TASKS = ["turn0", "out0", "v0", "stackq0", "stackk0", "qk0", "ffn2", "ffn3", "ffn4", "ffn5", "turn1",
             "out1", "v1", "stackq1", "stackk1", "qk1", "turn2", "y0", "y1", "ffn0", "ffn1"]
    PREP = {"ffn2": 0, "ffn3": 1, "ffn4": 2, "ffn5": 3, "turn2": 4, "y0": 5, "y1": 6, "ffn0": 7, "ffn1": 8}
    NBANK = 3

    def exists(p, task):
        if task in PREP and p == 0:
            return True
        if task in ("ffn2", "ffn3", "ffn4", "ffn5", "y0", "y1"):
            return 0 <= p - 2 < PAIRS
        if task in ("turn2", "ffn0", "ffn1"):
            return 0 <= p - 1 < PAIRS
        b = 2 * p + int(task[-1])
        ahead = {"out": -1, "sta": 1, "v": 1, "v0": 1, "v1": 1, "tur": 2, "qk0": 2, "qk1": 2}[task[:3]]
        return 0 <= b + ahead < B

    FIRST, FIRST_STEADY, LAST_STEADY = -1, 2, PAIRS - 3

    def use(p, task):
        pos = TASKS.index(task)
        q = p if isinstance(p, int) else FIRST_STEADY
        n = sum(exists(i, t) for i in range(FIRST, q + 1) for k, t in enumerate(TASKS)
                if k % NBANK == pos % NBANK and (i < q or k <= pos))
        return pos % NBANK, n if isinstance(p, int) else n + len(TASKS) // NBANK * (p - FIRST_STEADY)

    BATCHES = ((0, 1), (1, 4), (4, B))

    def since(v, least):
        return v >= least if isinstance(v, int) else True

    with ExitStack() as stack:
        def sb(name, shape, dt=F32):
            return stack.enter_context(nc.sbuf_tensor(name, shape, dt))

        def sem(name):
            return stack.enter_context(nc.semaphore(name))

        x_all = sb("x_all", [P, B, D])
        ctx_sb = sb("ctx_sb", [P, 2, D])
        w_raw = sb("w_raw", [P, 3, KC, D])
        w_hi = sb("w_hi", [P, KC, 3 * D], F32R)
        w_lo = sb("w_lo", [P, KC, 3 * D], F32R)
        gu_int = sb("gu_int", [P, 2, NJ, D], I32)
        dn_int = sb("dn_int", [P, KC, HID], I32)
        gu_raw = sb("gu_raw", [P, 2, NJ, D])
        dn_raw = sb("dn_raw", [P, KC, HID])
        gu_hi = sb("gu_hi", [P, NJ, 2, KC, P], F32R)
        gu_lo = sb("gu_lo", [P, NJ, 2, KC, P], F32R)
        dn_hi = sb("dn_hi", [P, NJ, D], F32R)
        dn_lo = sb("dn_lo", [P, NJ, D], F32R)
        minus_zero_point = sb("minus_zero_point", [P, 1])
        weight_max = sb("weight_max", [P, 6])
        weight_max_row = sb("weight_max_row", [1, P])
        wide_max = sb("wide_max", [1, 1])
        wide = sb("wide", [1, 1], I32)
        scales = sb("scales", [P, 3, NJ])
        half_gate = sb("half_gate", [P, NJ])
        down_scale = sb("down_scale", [P, D])
        gates = sb("gates", [P, 2])
        tanh_gates = sb("tanh_gates", [P, 2])
        ident = sb("ident", [P, P])
        ident16 = sb("ident16", [P, P], F16)
        x_stats = sb("x_stats", [P, B, 6])
        x_mean_var = sb("x_mean_var", [P, B, 2])
        x1_stats = sb("x1_stats", [P, 6])
        x1_mean_var = sb("x1_mean_var", [P, 2])
        x_bias = sb("x_bias", [P, B])
        x1_bias = sb("x1_bias", [P, 1])
        xn = sb("xn", [P, 2, D])
        x1n = sb("x1n", [P, 2, D])
        x_root = [sb(f"x_root_{part}", [P, B]) for part in ("in", "y", "xy", "v", "p")]
        root = [sb(f"root_{part}", [P, 2 * H + 1]) for part in ("in", "y", "xy", "v", "p")]
        root_in, root_y = root[0:2]
        xc_hi = sb("xc_hi", [P, 2, 2 * KC, P], F32R)
        xc_lo = sb("xc_lo", [P, 2, 2 * KC, P], F32R)
        squares = sb("squares", [P, 2 * D])
        qk_raw = sb("qk_raw", [P, 2 * H, HD])
        sums = sb("sums", [P, 2 * H])
        qk_unit = sb("qk_unit", [P, 2 * H, HD])
        qk_parts = sb("qk_parts", [P, 2 * H, 4, HD], F16)
        q_stack = sb("q_stack", [P, 2, GROUPS, P], F16)
        k_stack = sb("k_stack", [P, 2, GROUPS, P], F16)
        k_masked = sb("k_masked", [P, 2, 4, GROUPS, P], F16)
        v_blocks = sb("v_blocks", [P, 2, H * BLOCK])
        probs = sb("probs", [P, 2, HEADS_PER_OCTET * P])
        o_turned = sb("o_turned", [P, 2, 3 * P])
        inv_den = sb("inv_den", [P, 12, 3])
        attn = sb("attn", [P, D])
        x2_hi = sb("x2_hi", [P, KC, TOK], F32R)
        x2_lo = sb("x2_lo", [P, KC, TOK], F32R)
        tanh_g = sb("tanh_g", [P, 2, TOK])
        silu2 = sb("silu2", [P, 2, TOK])
        hidden = sb("hidden", [P, 3, TOK])
        h_hi = sb("h_hi", [P, NJ, TOK], F32R)
        h_lo = sb("h_lo", [P, NJ, TOK], F32R)
        y_sb = sb("y_sb", [P, 2, D])

        score_ps = [stack.enter_context(nc.psum_tensor(f"score_ps{i}", [P, HEADS_PER_OCTET, P], F32)) for i in range(2)]
        pv_ps = stack.enter_context(nc.psum_tensor("pv_ps", [P, 512], F32))
        bank = [stack.enter_context(nc.psum_tensor(f"bank{i}", [P, 512], F32)) for i in range(NBANK)]

        w_loaded = [sem(f"w_loaded{i}") for i in range(2)]
        x_loaded = [sem(f"x_loaded{i}") for i in range(3)]
        ctx_loaded = [sem(f"ctx_loaded{i}") for i in range(2)]
        ffn_w_loaded = sem("ffn_w_loaded")
        small_loaded = sem("small_loaded")
        km_loaded = [sem(f"km_loaded{i}") for i in range(2)]
        stored = sem("stored")
        ident_zeroed = sem("ident_zeroed")
        ident_ready = sem("ident_ready")
        ident16_ready = sem("ident16_ready")
        km_zeroed = sem("km_zeroed")
        first_keys_ready = sem("first_keys_ready")
        minus_ready = sem("minus_ready")
        v_zeroed = sem("v_zeroed")
        v_ready_ones = sem("v_ready_ones")
        tanh_ready = sem("tanh_ready")
        scale_steps = sem("scale_steps")
        w_converted = sem("w_converted")
        w_max_steps = sem("w_max_steps")
        w_max_row_loaded = sem("w_max_row_loaded")
        w_turned = sem("w_turned")
        w_hi_ready = sem("w_hi_ready")
        w_lo_ready = sem("w_lo_ready")
        prep_hi = sem("prep_hi")
        filled = [sem(f"filled{i}") for i in range(NBANK)]
        drained = [sem(f"drained{i}") for i in range(NBANK)]
        ctx_turned = sem("ctx_turned")
        x_stats_ready = sem("x_stats_ready")
        x_mean_ready = sem("x_mean_ready")
        x_eps_added = sem("x_eps_added")
        x_root_steps = sem("x_root_steps")
        x_bias_ready = sem("x_bias_ready")
        x1_bias_ready = sem("x1_bias_ready")
        xn_ready = sem("xn_ready")
        stats2_ready = sem("stats2_ready")
        mean2_ready = sem("mean2_ready")
        x1n_ready = sem("x1n_ready")
        eps_added = sem("eps_added")
        root_in_ready = sem("root_in_ready")
        root_steps = sem("root_steps")
        xc_hi_ready = sem("xc_hi_ready")
        squares_ready = sem("squares_ready")
        sums_ready = sem("sums_ready")
        unit_ready = sem("unit_ready")
        qk_hi_ready = sem("qk_hi_ready")
        qk_lo_ready = sem("qk_lo_ready")
        qk_parts_ready = sem("qk_parts_ready")
        scores_ready = sem("scores_ready")
        probs_ready = sem("probs_ready")
        pv_done = sem("pv_done")
        o_turned_ready = sem("o_turned_ready")
        inv_den_ready = sem("inv_den_ready")
        x1_ready = sem("x1_ready")
        x2_hi_ready = sem("x2_hi_ready")
        tanh_g_ready = sem("tanh_g_ready")
        silu2_ready = sem("silu2_ready")
        h_hi_ready = sem("h_hi_ready")
        h_lo_ready = sem("h_lo_ready")
        y_scaled = sem("y_scaled")
        last_y_scaled = sem("last_y_scaled")
        result_ready = sem("result_ready")

        def tile_of(b):
            if isinstance(b, int):
                return x_all[:, b, :]
            return x_all[:, bass.ds(b, 1), :].rearrange("p a d -> p (a d)")

        def dram_tile(t, b):
            if isinstance(b, int):
                return t[b]
            return t[bass.ds(b, 1)].rearrange("a s d -> (a s) d")

        def w_transposed(m):
            return score_ps[m % 2][:, 0:4, :] if m < 2 else score_ps[0][:, 4:8, :]

        def head_view(n, part):
            per, first, count = ((3, 0, 8), (2, 24, 4))[part]
            return bass.AP(v_blocks, (n * H + first) * BLOCK,
                           [[2 * H * BLOCK, P], [per * BLOCK, count], [BLOCK + SLOTW, per], [1, HD]])

        def first_keys(quadrant):
            rows_of = slice(BLOCK * quadrant, BLOCK * (quadrant + 1))
            k, _ = use(FIRST, "stackk1")
            return (k_masked[rows_of, 0, quadrant, :, :].rearrange("p g n -> p (g n)"), bank[k][rows_of, :].bitcast(F16))

        def run(eng, iteration, first=FIRST):
            for p in range(first, FIRST_STEADY):
                iteration(p)
            with eng.Fori(FIRST_STEADY, LAST_STEADY + 1) as p:
                iteration(p)
            for p in range(LAST_STEADY + 1, PAIRS + 2):
                iteration(p)

        def here(p, task):
            return exists(p, task) if isinstance(p, int) else True

        def has_tile(p, b):
            return 0 <= b < B if isinstance(p, int) else True

        def ending(p):
            return isinstance(p, int) and p >= PAIRS - 1

        def has_roots(p, b):
            return -2 <= b <= B if isinstance(p, int) else True

        block = stack.enter_context(nc.Block())

        @block.sync
        def _(sp):
            sp.dma_start(x_all[:, 0, :], x[0]).then_inc(x_loaded[0], 16)
            sp.dma_start(w_raw[:, 0, :, :], Wq.rearrange("(c p) d -> p c d", p=P)).then_inc(w_loaded[0], 16)
            sp.dma_start(ctx_sb[:, 0, :], ctx[0]).then_inc(ctx_loaded[0], 16)
            for c, w in enumerate((Wk, Wv)):
                both = w.rearrange("(p two) d -> p two d", two=2)
                sp.dma_start(w_raw[:, 1:3, c, :], both).then_inc(w_loaded[1], 16)
            sp.dma_start(x_all[:, 1:4, :], x[1:4].rearrange("b p d -> p b d")).then_inc(x_loaded[1], 16)
            sp.dma_start(ctx_sb[:, 1, :], ctx[1]).then_inc(ctx_loaded[1], 16)
            sp.dma_start(gates[:, 0:1], g_xattn.rearrange("(a d) -> a d", a=1).to_broadcast([P, 1])).then_inc(small_loaded, 16)
            sp.dma_start(gates[:, 1:2], g_ffn.rearrange("(a d) -> a d", a=1).to_broadcast([P, 1])).then_inc(small_loaded, 16)
            sp.dma_start(down_scale[:], s_down.rearrange("(a d) -> a d", a=1).to_broadcast([P, D])).then_inc(small_loaded, 16)
            full = (NJ - 1) * P
            for k, s in enumerate((s_gate, s_up)):
                with nc.allow_non_contiguous_dma(reason="704 scales, one to a partition"):
                    sp.dma_start(scales[:, k, 0:NJ - 1], s[0:full].rearrange("(j p) -> p j", p=P)).then_inc(small_loaded, 16)
                sp.dma_start(scales[0:LAST, k, NJ - 1:NJ], s[full:HID].rearrange("(p j) -> p j", j=1)).then_inc(small_loaded, 16)
            for k, w in enumerate((wq_gate, wq_up)):
                sp.dma_start(gu_int[:, k, 0:NJ - 1, :], w[0:full, :].rearrange("(j p) d -> p j d", p=P)).then_inc(ffn_w_loaded, 16)
                sp.dma_start(gu_int[0:LAST, k, NJ - 1, :], w[full:HID, :]).then_inc(ffn_w_loaded, 16)
            sp.dma_start(dn_int[:], wq_down.rearrange("(c p) h -> p c h", p=P)).then_inc(ffn_w_loaded, 16)
            sp.dma_start(x_all[:, 4:B, :], x[4:B].rearrange("b p d -> p b d")).then_inc(x_loaded[2], 16)

            def iteration(p):
                for e in range(2):
                    b = 2 * p + e
                    if has_tile(p, b + 1) and since(b, 0):
                        n = 1 - e
                        k, m = use(p, f"stackk{e}")
                        sp.wait_ge(drained[k], m)
                        if not since(b, 1):
                            sp.wait_ge(km_zeroed, 1)
                        for j in range(4):
                            sp.dma_start(k_masked[BLOCK * j:BLOCK * (j + 1), n, j, :, :],
                                         k_stack[BLOCK * j:BLOCK * (j + 1), n, :, :]).then_inc(km_loaded[n], 16)
                    if has_tile(p, b + 2) and has_tile(p, b + 4):
                        sp.wait_ge(ctx_turned, b + 3)
                        sp.dma_start(ctx_sb[:, e, :], dram_tile(ctx, b + 4)).then_inc(ctx_loaded[e], 16)
                    if isinstance(p, int) and p == 0 and e == 1:
                        sp.wait_ge(w_max_steps, 6)
                        sp.dma_start(weight_max_row[:], weight_max[:, 5:6]).then_inc(w_max_row_loaded, 16)
                    if e == 1 and (not isinstance(p, int) or p >= 2):
                        for k in range(2):
                            done = 2 * (p - 2) + k
                            sp.wait_ge(result_ready, done + 3)
                            sp.dma_start(dram_tile(out, done), tile_of(done)).then_inc(stored, 16)

            run(sp, iteration)
            sp.wait_ge(stored, 16 * B)

        @block.gpsimd
        def _(pool):
            nc.gpsimd.memset(ident[:], 0.0).then_inc(ident_zeroed, 1)
            pool.wait_ge(ident_zeroed, 1)
            nc.gpsimd.affine_select(out=ident[:], in_=ident[:], compare_op=ALU.not_equal, fill=1.0, base=0,
                                    pattern=[[-1, P]], channel_multiplier=1).then_inc(ident_ready, 1)
            pool.wait_ge(ident_ready, 1)
            nc.gpsimd.tensor_copy(ident16[:], ident[:]).then_inc(ident16_ready, 1)

            nc.gpsimd.memset(v_blocks[:], 0.0).then_inc(v_zeroed, 1)
            nc.gpsimd.memset(k_masked[:].bitcast(F32), 0.0).then_inc(km_zeroed, 1)
            pool.wait_ge(v_zeroed, 1)
            for e in range(2):
                v = v_blocks[:, e, 0:24 * BLOCK].rearrange("p (t c) -> p t c", c=3 * BLOCK)
                for i in range(3):
                    nc.gpsimd.memset(v[:, :, i * (BLOCK + SLOTW) + HD:i * (BLOCK + SLOTW) + HD + 1], 1.0)
                w = v_blocks[:, e, 24 * BLOCK:].rearrange("p (t c) -> p t c", c=2 * BLOCK)
                for i in range(2):
                    nc.gpsimd.memset(w[:, :, i * (BLOCK + SLOTW) + HD:i * (BLOCK + SLOTW) + HD + 1], 1.0)
                last = nc.gpsimd.memset(w[:, :, 3 * SLOTW - 1:3 * SLOTW], 1.0)
            last.then_inc(v_ready_ones, 1)
            nc.gpsimd.memset(y_sb[:, 0, :], 0.0).then_inc(result_ready, 1)
            nc.gpsimd.memset(y_sb[:, 1, :], 0.0).then_inc(result_ready, 1)

            def split_qk(p, e):
                b = 2 * p + e
                if not has_tile(p, b + 2):
                    return
                pool.wait_ge(qk_hi_ready, b + 3)
                nc.gpsimd.tensor_tensor(qk_parts[:, :, 1, :], qk_unit[:], qk_parts[:, :, 0, :],
                                        ALU.subtract).then_inc(qk_lo_ready, 1)

            def split_hidden(p, q, j):
                n = NJ * (p - q) + j
                pool.wait_ge(h_hi_ready, n + 1)
                r = rows(j)
                nc.gpsimd.tensor_tensor(h_lo[0:r, j, :], hidden[0:r, j % 3, :], h_hi[0:r, j, :].bitcast(F32),
                                        ALU.subtract).then_inc(h_lo_ready, 1)

            def add_attention(p, e):
                b = 2 * p + e - 1
                if has_tile(p, b):
                    k, n = use(p, f"out{e}")
                    pool.wait_ge(drained[k], n)
                    nc.gpsimd.tensor_tensor(tile_of(b), tile_of(b), attn[:], ALU.add).then_inc(x1_ready, 1)

            def add_y(p, e):
                if isinstance(p, int) and p == PAIRS + 1:
                    return
                done = 2 * (p - 2) + e
                k, n = use(p, f"y{e}")
                pool.wait_ge(drained[k], n)
                nc.gpsimd.tensor_tensor(y_sb[:, e, :], y_sb[:, e, :], down_scale[:], ALU.mult).then_inc(y_scaled, 1)
                pool.wait_ge(y_scaled, done + 1)
                nc.gpsimd.tensor_tensor(tile_of(done), tile_of(done), y_sb[:, e, :], ALU.add).then_inc(result_ready, 1)

            def qk_norm(p, e):
                b = 2 * p + e
                if not has_tile(p, b + 2):
                    return
                pool.wait_ge(root_steps, (ROOT_STEPS + 1) * (b + 3))
                k, m = use(p, f"qk{e}")
                pool.wait_ge(drained[k], m)
                if since(b, -1):
                    pool.wait_ge(qk_lo_ready, b + 2)
                nc.gpsimd.tensor_tensor(qk_unit[:], qk_raw[:], root_y[:, 0:2 * H].unsqueeze(2).to_broadcast([P, 2 * H, HD]),
                                        ALU.mult).then_inc(unit_ready, 1)

            def real(p, task):
                return here(p, task) and not (isinstance(p, int) and p == 0)

            def split_chunks(p, q, chunks):
                if real(p, f"ffn{chunks[0]}"):
                    for j in chunks:
                        split_hidden(p, q, j)

            def iteration(p):
                add_attention(p, 0)
                split_chunks(p - 1, 1, (0, 1))
                qk_norm(p, 0)
                split_chunks(p, 2, (2,))
                split_qk(p, 0)
                split_chunks(p, 2, (3, 4, 5))
                add_attention(p, 1)
                qk_norm(p, 1)
                split_qk(p, 1)
                if real(p, "y0"):
                    add_y(p, 0)
                    add_y(p, 1)

            run(pool, iteration)

        @block.scalar
        def _(act):
            def upper_weight(m):
                act.wait_ge(w_turned, m + 1)
                nc.scalar.copy(w_hi[:, :, m * D:(m + 1) * D], w_transposed(m).rearrange("p (k a) n -> p k (a n)", k=KC)
                               ).then_inc(w_hi_ready, 1)

            def convert_gate_up():
                act.wait_ge(minus_ready, 1)
                act.wait_ge(ffn_w_loaded, 16 * 5)
                for k in range(2):
                    nc.scalar.activation(gu_raw[:, k, 0:NJ - 1, :], gu_int[:, k, 0:NJ - 1, :], ACT.Identity,
                                         bias=minus_zero_point[:])
                    nc.scalar.activation(gu_raw[0:LAST, k, NJ - 1, :], gu_int[0:LAST, k, NJ - 1, :], ACT.Identity,
                                         bias=minus_zero_point[0:LAST, :])

            def convert_down():
                nc.scalar.activation(dn_raw[:], dn_int[:], ACT.Identity, bias=minus_zero_point[:]).then_inc(w_converted, 1)

            def exp_octet(p, e, t):
                b = 2 * p + e
                o = OCTETS * b + t
                if not has_tile(p, b):
                    return
                act.wait_ge(scores_ready, o + 1)
                if since(o, 2):
                    act.wait_ge(pv_done, o - 1)
                nc.scalar.activation(probs[:, t % 2, :], score_ps[t % 2][:].rearrange("p h n -> p (h n)"),
                                     ACT.Exp, scale=float(HD) ** 0.5 / UNIT ** 2).then_inc(probs_ready, 1)

            def drain_pv(p, e):
                b = 2 * p + e
                if has_tile(p, b - 1):
                    act.wait_ge(pv_done, OCTETS * b)
                    nc.scalar.copy(o_turned[:, 1 - e, :], pv_ps[:, 0:3 * P]).then_inc(o_turned_ready, 1)

            def drain_v(p, e):
                b = 2 * p + e
                if not has_tile(p, b + 1):
                    return
                n = 1 - e
                k, m = use(p, f"v{e}")
                act.wait_ge(filled[k], m)
                if not since(b, 0):
                    act.wait_ge(v_ready_ones, 1)
                    act.wait_ge(tanh_ready, 1)
                src = bank[k][:, 0:24 * HD].rearrange("p (t i d) -> p t i d", i=3, d=HD)
                nc.scalar.activation(head_view(n, 0), src, ACT.Identity, scale=tanh_gates[:, 0:1])
                src = bank[k][:, 24 * HD:D].rearrange("p (t i d) -> p t i d", i=2, d=HD)
                nc.scalar.activation(head_view(n, 1), src, ACT.Identity, scale=tanh_gates[:, 0:1]).then_inc(drained[k], 1)

            def turn_hi(p, e):
                b = 2 * p + e
                if has_tile(p, b + 2):
                    k, m = use(p, f"turn{e}")
                    act.wait_ge(filled[k], m)
                    nc.scalar.copy(xc_hi[:, e, :, :].rearrange("p a n -> p (a n)"), bank[k][:]).then_inc(xc_hi_ready, 1)

            def stack_keys(p, e):
                b = 2 * p + e
                if has_tile(p, b + 1):
                    k, m = use(p, f"stackk{e}")
                    act.wait_ge(filled[k], m)
                    nc.scalar.copy(k_stack[:, 1 - e, :, :].rearrange("p g n -> p (g n)"),
                                   bank[k][:].bitcast(F16)).then_inc(drained[k], 1)

            def mask_first_keys():
                k, m = use(FIRST, "stackk1")
                act.wait_ge(filled[k], m)
                act.wait_ge(km_zeroed, 1)
                for quadrant in range(2):
                    if quadrant == 1:
                        act.wait_ge(first_keys_ready, 1)
                    last = nc.scalar.copy(*first_keys(quadrant))
                last.then_inc(drained[k], 1)

            def square(p, e):
                b = 2 * p + e
                if has_tile(p, b + 2):
                    k, m = use(p, f"qk{e}")
                    act.wait_ge(filled[k], m)
                    if since(b, -1):
                        act.wait_ge(sums_ready, b + 2)
                    nc.scalar.activation(squares[:], bank[k][:], ACT.Square).then_inc(squares_ready, 1)

            def copy_qk(p, e):
                b = 2 * p + e
                if has_tile(p, b + 2):
                    k, m = use(p, f"qk{e}")
                    act.wait_ge(filled[k], m)
                    if since(b, -1):
                        act.wait_ge(unit_ready, b + 2)
                    nc.scalar.copy(qk_raw[:].rearrange("p h d -> p (h d)"), bank[k][:]).then_inc(drained[k], 1)

            def normalize(p, e):
                b = 2 * p + e + 3
                if not has_tile(p, b):
                    return
                if isinstance(b, int):
                    batch = 1 + [b < last for first, last in BATCHES].index(True)
                    act.wait_ge(x_bias_ready, batch)
                    one = slice(b, b + 1)
                else:
                    one = bass.ds(b, 1)
                if since(b, 2):
                    k, m = use(p, "turn0") if e else use(p - 1, "turn1")
                    act.wait_ge(filled[k], m)
                nc.scalar.activation(xn[:, 1 - e, :], tile_of(b), ACT.Identity, bias=x_bias[:, one],
                                     scale=x_root[1][:, one]).then_inc(xn_ready, 1)

            def normalize2(p, e):
                b = 2 * p + e - 1
                if not has_tile(p, b):
                    return
                act.wait_ge(x1_bias_ready, b + 1)
                if since(b, 2):
                    k, m = use(p if e else p - 1, "turn2")
                    act.wait_ge(filled[k], m)
                nc.scalar.activation(x1n[:, 1 - e, :], tile_of(b), ACT.Identity, bias=x1_bias[:], scale=root_y[:, 2 * H:]).then_inc(x1n_ready, 1)

            def drain_y(p, e):
                task = f"y{e}"
                if not here(p, task):
                    return
                k, m = use(p, task)
                if isinstance(p, int) and p == 0:
                    prep(task, k, m)
                    return
                if isinstance(p, int) and p == PAIRS + 1:
                    return
                done = 2 * (p - 2) + e
                act.wait_ge(filled[k], m)
                act.wait_ge(result_ready, done + 1)
                nc.scalar.copy(y_sb[:, e, :], bank[k][:, 0:D]).then_inc(drained[k], 1)

            def tanh_chunk(p, q, j):
                task = f"ffn{j}"
                if not here(p, task):
                    return
                k, m = use(p, task)
                if isinstance(p, int) and p == 0:
                    prep(task, k, m)
                    return
                n = NJ * (p - q) + j
                act.wait_ge(filled[k], m)
                if isinstance(n, int) and n == 0:
                    act.wait_ge(scale_steps, 2)
                if since(n, 2):
                    act.wait_ge(silu2_ready, n - 1)
                r = rows(j)
                nc.scalar.activation(tanh_g[0:r, j % 2, :], bank[k][0:r, 0:TOK], ACT.Tanh,
                                     scale=half_gate[0:r, j:j + 1]).then_inc(tanh_g_ready, 1)

            def upper(p, q, j):
                task = f"ffn{j}"
                if not here(p, task) or isinstance(p, int) and p == 0:
                    return
                k, m = use(p, task)
                r = rows(j)
                act.wait_ge(drained[k], m)
                nc.scalar.copy(h_hi[0:r, j, :], hidden[0:r, j % 3, :]).then_inc(h_hi_ready, 1)

            def prep(task, k, m):
                part = PREP[task]
                act.wait_ge(filled[k], m)
                if part < NJ:
                    nc.scalar.copy(gu_hi[:, part, :, :, 0:rows(part)],
                                   bank[k][:].rearrange("p (a c n) -> p a c n", a=2, c=KC)[:, :, :, 0:rows(part)]
                                   ).then_inc(prep_hi, 1)
                    return
                for a in range(2):
                    j = 2 * (part - NJ) + a
                    last = nc.scalar.copy(dn_hi[0:rows(j), j, :], bank[k][0:rows(j), a * D:(a + 1) * D])
                last.then_inc(prep_hi, 1)

            def turn2_hi(p):
                if not here(p, "turn2"):
                    return
                k, m = use(p, "turn2")
                if isinstance(p, int) and p == 0:
                    prep("turn2", k, m)
                    return
                act.wait_ge(filled[k], m)
                nc.scalar.copy(x2_hi[:].rearrange("p c n -> p (c n)"), bank[k][:]).then_inc(x2_hi_ready, 1)

            def begin(p):
                first = isinstance(p, int) and p == FIRST
                drain_pv(p, 0)
                exp_octet(p, 0, 0)
                turn_hi(p, 0)
                if first:
                    upper_weight(2)
                    act.wait_ge(small_loaded, 16 * 7)
                    nc.scalar.activation(tanh_gates[:], gates[:], ACT.Tanh).then_inc(tanh_ready, 1)
                exp_octet(p, 0, 1)
                drain_v(p, 0)
                if not first:
                    normalize(p, 0)
                upper(p - 1, 1, 0)
                if isinstance(p, int) and p == PAIRS + 1:
                    tanh_chunk(p, 2, 2)
                upper(p - 1, 1, 1)
                stack_keys(p, 0)

            def iteration(p):
                first = isinstance(p, int) and p == FIRST
                square(p, 0)
                exp_octet(p, 0, 2)
                copy_qk(p, 0)
                if first:
                    normalize(p, 0)
                if not (isinstance(p, int) and p == PAIRS + 1):
                    tanh_chunk(p, 2, 2)
                tanh_chunk(p, 2, 3)
                exp_octet(p, 0, 3)
                upper(p, 2, 2)
                if isinstance(p, int) and p == PAIRS - 1:
                    normalize2(p, 0)
                tanh_chunk(p, 2, 4)
                if ending(p):
                    upper(p, 2, 3)
                drain_pv(p, 1)
                exp_octet(p, 1, 0)
                tanh_chunk(p, 2, 5)
                if isinstance(p, int) and p == PAIRS:
                    normalize2(p, 0)
                turn_hi(p, 1)
                exp_octet(p, 1, 1)
                if not ending(p):
                    upper(p, 2, 3)
                    normalize2(p, 0)
                upper(p, 2, 4)
                drain_v(p, 1)
                upper(p, 2, 5)
                if first:
                    convert_gate_up()
                    square(p, 1)
                    copy_qk(p, 1)
                    convert_down()
                    mask_first_keys()
                    normalize(p, 1)
                else:
                    stack_keys(p, 1)
                    normalize(p, 1)
                    square(p, 1)
                    copy_qk(p, 1)
                exp_octet(p, 1, 2)
                turn2_hi(p)
                drain_y(p, 0)
                exp_octet(p, 1, 3)
                if not (isinstance(p, int) and p == 0):
                    normalize2(p, 1)
                drain_y(p, 1)
                tanh_chunk(p, 1, 0)
                tanh_chunk(p, 1, 1)
                if isinstance(p, int) and p == 0:
                    normalize2(p, 1)
                begin(p + 1)

            upper_weight(0)
            normalize(-2, 1)
            upper_weight(1)
            begin(FIRST)
            run(act, iteration)

        @block.vector
        def _(dve):
            nc.vector.memset(root_in[:], 1.0)
            nc.vector.memset(weight_max[:], 0.0)
            nc.vector.memset(minus_zero_point[:], -ZERO_POINT).then_inc(minus_ready, 1)

            def root_chain(buffers, cols, count, before, first=1, last=ROOT_STEPS):
                r_in, y, xy, v, q = (b[:, cols] for b in buffers)
                stt = nc.vector.scalar_tensor_tensor
                steps = (
                    lambda: stt(out=xy, in0=r_in, scalar=-1.0, in1=y, op0=ALU.mult, op1=ALU.mult),
                    lambda: stt(out=v, in0=xy, scalar=1.0, in1=y, op0=ALU.mult, op1=ALU.mult),
                    lambda: stt(out=y, in0=v, scalar=3 * START_SCALE ** 2, in1=y, op0=ALU.add, op1=ALU.mult),
                    lambda: stt(out=xy, in0=r_in, scalar=1.0, in1=y, op0=ALU.mult, op1=ALU.mult),
                    lambda: stt(out=v, in0=xy, scalar=1.0, in1=y, op0=ALU.mult, op1=ALU.mult),
                    lambda: stt(out=q, in0=v, scalar=-10 / 3 * MID_SCALE ** 2, in1=v, op0=ALU.add, op1=ALU.mult),
                    lambda: stt(out=y, in0=q, scalar=5 * MID_SCALE ** 4, in1=y, op0=ALU.add, op1=ALU.mult),
                )
                for n in range(first, last + 1):
                    dve.wait_ge(count, before + n)
                    steps[n - 1]().then_inc(count, 1)

            def x_statistics(i, first, last):
                dve.wait_ge(x_loaded[i], 16)
                for b in range(first, last):
                    nc.vector.bn_stats(x_stats[:, b, :], x_all[:, b, :]).then_inc(x_stats_ready, 1)

            def x_means(i):
                first, last = BATCHES[i]
                dve.wait_ge(x_stats_ready, last)
                for b in range(first, last):
                    nc.vector.bn_aggr(x_mean_var[:, b, :], x_stats[:, b, :]).then_inc(x_mean_ready, 1)
                dve.wait_ge(x_mean_ready, last)
                nc.vector.tensor_scalar(x_root[0][:, first:last], x_mean_var[:, first:last, 1], LN_EPS, None,
                                        ALU.add).then_inc(x_eps_added, 1)
                dve.wait_ge(x_eps_added, i + 1)
                nc.vector.tensor_scalar(x_root[1][:, first:last].bitcast(I32), x_root[0][:, first:last].bitcast(I32), -0.5,
                                        START_BITS, ALU.mult, ALU.add).then_inc(x_root_steps, 1)

            def x_roots(i, first=1, last=ROOT_STEPS):
                root_chain(x_root, slice(*BATCHES[i]), x_root_steps, (ROOT_STEPS + 1) * i, first, last)

            def x_offsets(i):
                first, last = BATCHES[i]
                dve.wait_ge(x_root_steps, (ROOT_STEPS + 1) * (i + 1))
                nc.vector.scalar_tensor_tensor(out=x_bias[:, first:last], in0=x_mean_var[:, first:last, 0], scalar=-1.0,
                                               in1=x_root[1][:, first:last], op0=ALU.mult, op1=ALU.mult).then_inc(x_bias_ready, 1)

            def lower_weight(m):
                dve.wait_ge(w_hi_ready, m + 1)
                nc.vector.tensor_tensor(w_lo[:, :, m * D:(m + 1) * D], w_transposed(m).rearrange("p (k a) n -> p k (a n)", k=KC),
                                        w_hi[:, :, m * D:(m + 1) * D].bitcast(F32), ALU.subtract).then_inc(w_lo_ready, 1)

            x_statistics(0, 0, 1)
            x_means(0)
            x_roots(0)
            x_offsets(0)
            lower_weight(0)
            lower_weight(1)

            def wait_for_root_buffers(p, b):
                if has_tile(p, b - 1):
                    dve.wait_ge(stats2_ready, b)
                if since(b, -1) and has_tile(p, b + 1):
                    dve.wait_ge(unit_ready, b + 2)
                if since(b, 2):
                    dve.wait_ge(x1n_ready, b - 1)

            def root_inputs(p, e):
                b = 2 * p + e
                if not has_roots(p, b):
                    return
                if not has_tile(p, b + 2):
                    wait_for_root_buffers(p, b)
                if has_tile(p, b - 1):
                    nc.vector.bn_aggr(x1_mean_var[:], x1_stats[:]).then_inc(mean2_ready, 1)
                    dve.wait_ge(mean2_ready, b)
                    nc.vector.tensor_scalar(root_in[:, 2 * H:], x1_mean_var[:, 1:2], LN_EPS, None, ALU.add).then_inc(root_in_ready, 1)
                if has_tile(p, b + 2):
                    dve.wait_ge(sums_ready, b + 3)
                    nc.vector.tensor_scalar(root_in[:, 0:2 * H], sums[:], HD * RMS_EPS, UNIT ** -2, ALU.add, ALU.mult).then_inc(eps_added, 1)
                if has_tile(p, b - 1):
                    dve.wait_ge(root_in_ready, b)
                if has_tile(p, b + 2):
                    dve.wait_ge(eps_added, b + 3)
                nc.vector.tensor_scalar(root_y[:].bitcast(I32), root_in[:].bitcast(I32), -0.5, START_BITS, ALU.mult,
                                        ALU.add).then_inc(root_steps, 1)

            def x1_offset(p, e):
                b = 2 * p + e
                if has_tile(p, b - 1):
                    dve.wait_ge(root_steps, (ROOT_STEPS + 1) * (b + 3))
                    nc.vector.scalar_tensor_tensor(out=x1_bias[:], in0=x1_mean_var[:, 0:1], scalar=-1.0, in1=root_y[:, 2 * H:],
                                                   op0=ALU.mult, op1=ALU.mult).then_inc(x1_bias_ready, 1)

            def roots(p, e, first, last):
                b = 2 * p + e
                if has_roots(p, b):
                    root_chain(root, slice(0, 2 * H + 1), root_steps, (ROOT_STEPS + 1) * (b + 2), first, last)

            def turn_lo(p, e):
                b = 2 * p + e
                if has_tile(p, b + 2):
                    k, m = use(p, f"turn{e}")
                    dve.wait_ge(filled[k], m)
                    dve.wait_ge(xc_hi_ready, b + 3)
                    nc.vector.tensor_tensor(xc_lo[:, e, :, :].rearrange("p a n -> p (a n)"), bank[k][:],
                                            xc_hi[:, e, :, :].rearrange("p a n -> p (a n)").bitcast(F32),
                                            ALU.subtract).then_inc(drained[k], 1)

            def sum_squares(p, e):
                b = 2 * p + e
                if has_tile(p, b + 2):
                    wait_for_root_buffers(p, b)
                    dve.wait_ge(squares_ready, b + 3)
                    nc.vector.tensor_reduce(sums[:], squares[:].rearrange("p (h d) -> p h d", d=HD), AX.X,
                                            ALU.add).then_inc(sums_ready, 1)

            def qk_upper(p, e):
                b = 2 * p + e
                if not has_tile(p, b + 2):
                    return
                dve.wait_ge(unit_ready, b + 3)
                if since(b, -1):
                    k, m = use(p, f"stackk{e}")
                    dve.wait_ge(filled[k], m)
                nc.vector.tensor_copy(qk_parts[:, :, 0, :], qk_unit[:]).then_inc(qk_hi_ready, 1)

            def qk_double(p, e):
                b = 2 * p + e
                if not has_tile(p, b + 1):
                    return
                dve.wait_ge(qk_lo_ready, b + 2)
                words = qk_parts[:].rearrange("p h a d -> p h (a d)").bitcast(F32)
                W = HD // 2
                nc.vector.tensor_copy(words[:, 0:H, 2 * W:4 * W], words[:, 0:H, 0:2 * W])
                nc.vector.tensor_copy(words[:, H:2 * H, 2 * W:3 * W], words[:, H:2 * H, W:2 * W])
                nc.vector.tensor_copy(words[:, H:2 * H, 3 * W:4 * W], words[:, H:2 * H, 0:W]).then_inc(qk_parts_ready, 1)

            def mask_first_keys():
                k, m = use(FIRST, "stackk1")
                dve.wait_ge(filled[k], m)
                dve.wait_ge(km_zeroed, 1)
                for quadrant in range(2, 4):
                    last = nc.vector.tensor_copy(*first_keys(quadrant))
                last.then_inc(first_keys_ready, 1)

            def stack_queries(p, e):
                b = 2 * p + e
                if has_tile(p, b + 1):
                    k, m = use(p, f"stackq{e}")
                    dve.wait_ge(filled[k], m)
                    nc.vector.tensor_copy(q_stack[:, 1 - e, :, :].rearrange("p g n -> p (g n)"),
                                          bank[k][:].bitcast(F16)).then_inc(drained[k], 1)

            def out_reciprocal(p, e):
                b = 2 * p + e - 1
                if has_tile(p, b):
                    k, m = use(p, f"out{e}")
                    dve.wait_ge(filled[k], m)
                    nc.vector.reciprocal(inv_den[:], out_slots(k)[:, :, :, HD]).then_inc(inv_den_ready, 1)

            def out_slots(k):
                blocks = bank[k][:, 0:3 * P].rearrange("p (t c) -> p t c", c=BLOCK)
                return blocks[:, :, 0:3 * SLOTW].rearrange("p t (i c) -> p t i c", c=SLOTW)

            def out_divide(p, e):
                b = 2 * p + e - 1
                if not has_tile(p, b):
                    return
                k, m = use(p, f"out{e}")
                dve.wait_ge(inv_den_ready, b + 1)
                if since(b, 1):
                    dve.wait_ge(x1_ready, b)
                for t0, t1, per, h0 in ((0, 8, 3, 0), (8, 12, 2, 24)):
                    dst = attn[:, h0 * HD:(h0 + (t1 - t0) * per) * HD].rearrange("p (t i d) -> p t i d", i=per, d=HD)
                    last = nc.vector.tensor_tensor(dst, out_slots(k)[:, t0:t1, 0:per, 0:HD],
                                                   inv_den[:, t0:t1, 0:per].unsqueeze(3).to_broadcast([P, t1 - t0, per, HD]),
                                                   ALU.mult)
                last.then_inc(drained[k], 1)

            def statistics2(p, e):
                b = 2 * p + e - 1
                if has_tile(p, b):
                    dve.wait_ge(x1_ready, b + 1)
                    nc.vector.bn_stats(x1_stats[:], tile_of(b)).then_inc(stats2_ready, 1)

            def gate(p, q, j):
                task = f"ffn{j}"
                if not here(p, task):
                    return
                k, m = use(p, task)
                if isinstance(p, int) and p == 0:
                    prep(task, k, m)
                    return
                n = NJ * (p - q) + j
                r = rows(j)
                if isinstance(n, int) and n == 0:
                    dve.wait_ge(scale_steps, 5)
                dve.wait_ge(tanh_g_ready, n + 1)
                nc.vector.scalar_tensor_tensor(out=silu2[0:r, j % 2, :], in0=tanh_g[0:r, j % 2, :], scalar=1.0,
                                               in1=bank[k][0:r, 0:TOK], op0=ALU.add, op1=ALU.mult).then_inc(silu2_ready, 1)

            def up(p, q, j):
                task = f"ffn{j}"
                if not here(p, task) or isinstance(p, int) and p == 0:
                    return
                k, m = use(p, task)
                n = NJ * (p - q) + j
                r = rows(j)
                dve.wait_ge(silu2_ready, n + 1)
                if since(n, 3):
                    dve.wait_ge(h_lo_ready, n - 1 if j == 2 and not isinstance(p, int) else n - 2)
                nc.vector.scalar_tensor_tensor(out=hidden[0:r, j % 3, :], in0=silu2[0:r, j % 2, :], scalar=scales[0:r, 2, j:j + 1],
                                               in1=bank[k][0:r, TOK:2 * TOK], op0=ALU.mult, op1=ALU.mult).then_inc(drained[k], 1)

            def prep(task, k, m):
                part = PREP[task]
                dve.wait_ge(filled[k], m)
                dve.wait_ge(prep_hi, part + 1)
                if part < NJ:
                    r = rows(part)
                    nc.vector.tensor_tensor(gu_lo[:, part, :, :, 0:r],
                                            bank[k][:].rearrange("p (a c n) -> p a c n", a=2, c=KC)[:, :, :, 0:r],
                                            gu_hi[:, part, :, :, 0:r].bitcast(F32), ALU.subtract).then_inc(drained[k], 1)
                    return
                for a in range(2):
                    j = 2 * (part - NJ) + a
                    last = nc.vector.tensor_tensor(dn_lo[0:rows(j), j, :], bank[k][0:rows(j), a * D:(a + 1) * D],
                                                   dn_hi[0:rows(j), j, :].bitcast(F32), ALU.subtract)
                last.then_inc(drained[k], 1)

            def turn2_lo(p):
                if not here(p, "turn2"):
                    return
                k, m = use(p, "turn2")
                if isinstance(p, int) and p == 0:
                    prep("turn2", k, m)
                    return
                dve.wait_ge(filled[k], m)
                dve.wait_ge(x2_hi_ready, p)
                nc.vector.tensor_tensor(x2_lo[:].rearrange("p c n -> p (c n)"), bank[k][:],
                                        x2_hi[:].rearrange("p c n -> p (c n)").bitcast(F32),
                                        ALU.subtract).then_inc(drained[k], 1)

            def prep_y(p, e):
                if isinstance(p, int) and p == 0:
                    prep(f"y{e}", *use(p, f"y{e}"))

            def add_last_pair():
                for e in range(2):
                    k, n = use(PAIRS + 1, f"y{e}")
                    dve.wait_ge(filled[k], n)
                    nc.vector.tensor_tensor(y_sb[:, e, :], bank[k][:, 0:D], down_scale[:], ALU.mult).then_inc(last_y_scaled, 1)
                for e in range(2):
                    done = B - 2 + e
                    dve.wait_ge(last_y_scaled, e + 1)
                    nc.vector.tensor_tensor(tile_of(done), tile_of(done), y_sb[:, e, :], ALU.add).then_inc(result_ready, 1)

            def scale_setup():
                dve.wait_ge(small_loaded, 16 * 7)
                for r, j0, j1 in ((P, 0, NJ - 1), (LAST, NJ - 1, NJ)):
                    nc.vector.tensor_scalar(half_gate[0:r, j0:j1], scales[0:r, 0, j0:j1], 0.5, None, ALU.mult).then_inc(scale_steps, 1)
                dve.wait_ge(scale_steps, 2)
                for r, j0, j1 in ((P, 0, NJ - 1), (LAST, NJ - 1, NJ)):
                    nc.vector.tensor_tensor(scales[0:r, 2, j0:j1], half_gate[0:r, j0:j1], scales[0:r, 1, j0:j1],
                                            ALU.mult).then_inc(scale_steps, 1)
                dve.wait_ge(tanh_ready, 1)
                nc.vector.tensor_scalar(down_scale[:], down_scale[:], tanh_gates[:, 1:2], None, ALU.mult).then_inc(scale_steps, 1)

            def widest_weight(part):
                dve.wait_ge(w_converted, 1)
                if part < 2:
                    nc.vector.tensor_reduce(weight_max[:, part:part + 1], gu_raw[:, part, 0:NJ - 1, :], AX.XY, ALU.max,
                                            apply_absolute_value=True).then_inc(w_max_steps, 1)
                    nc.vector.tensor_reduce(weight_max[0:LAST, 3 + part:4 + part], gu_raw[0:LAST, part, NJ - 1, :], AX.X, ALU.max,
                                            apply_absolute_value=True).then_inc(w_max_steps, 1)
                    return
                nc.vector.tensor_reduce(weight_max[:, 2:3], dn_raw[:], AX.XY, ALU.max, apply_absolute_value=True).then_inc(w_max_steps, 1)
                dve.wait_ge(w_max_steps, 5)
                nc.vector.tensor_reduce(weight_max[:, 5:6], weight_max[:, 0:5], AX.X, ALU.max).then_inc(w_max_steps, 1)

            def any_wide_weight():
                dve.wait_ge(w_max_row_loaded, 16)
                nc.vector.tensor_reduce(wide_max[:], weight_max_row[:], AX.X, ALU.max).then_inc(w_max_steps, 1)
                dve.wait_ge(w_max_steps, 7)
                nc.vector.tensor_scalar(wide[:], wide_max[:], F32R_INTEGERS, None, ALU.is_gt).then_inc(w_max_steps, 1)

            def begin(p):
                first = isinstance(p, int) and p == FIRST
                second = isinstance(p, int) and p == FIRST + 1
                out_reciprocal(p, 0)
                turn_lo(p, 0)
                if first:
                    lower_weight(2)
                    x_statistics(1, 1, 4)
                    x_means(1)
                    x_roots(1)
                    x_offsets(1)
                out_divide(p, 0)
                if second:
                    x_statistics(2, 10, B)
                stack_queries(p, 0)
                if second:
                    x_means(2)
                    widest_weight(0)
                if isinstance(p, int) and p == PAIRS:
                    gate(p, 2, 2)
                statistics2(p, 0)

            def iteration(p):
                first = isinstance(p, int) and p == FIRST
                second = isinstance(p, int) and p == FIRST + 1
                early = isinstance(p, int) and p == 0
                sum_squares(p, 0)
                root_inputs(p, 0)
                if isinstance(p, int) and p == PAIRS:
                    up(p, 2, 2)
                    roots(p, 0, 1, 2)
                    gate(p, 2, 3)
                    roots(p, 0, 3, 3)
                    up(p, 2, 3)
                    roots(p, 0, 4, 7)
                    x1_offset(p, 0)
                    gate(p, 2, 4)
                    up(p, 2, 4)
                elif second:
                    for n in range(1, ROOT_STEPS + 1):
                        roots(p, 0, n, n)
                        x_roots(2, n, n)
                    x_offsets(2)
                    gate(p, 2, 2)
                    gate(p, 2, 3)
                else:
                    roots(p, 0, 1, 5)
                    gate(p, 2, 2)
                    roots(p, 0, 6, 6)
                    up(p, 2, 2)
                    roots(p, 0, 7, 7)
                    gate(p, 2, 3)
                    x1_offset(p, 0)
                    up(p, 2, 3)
                if first:
                    turn_lo(p, 1)
                qk_upper(p, 0)
                if not (isinstance(p, int) and p == PAIRS):
                    gate(p, 2, 4)
                    up(p, 2, 4)
                gate(p, 2, 5)
                up(p, 2, 5)
                if not first:
                    turn_lo(p, 1)
                qk_double(p, 1)
                out_reciprocal(p, 1)
                out_divide(p, 1)
                if first:
                    scale_setup()
                    sum_squares(p, 1)
                    root_inputs(p, 1)
                    stack_queries(p, 1)
                    roots(p, 1, 1, 2)
                    mask_first_keys()
                    roots(p, 1, 3, 4)
                else:
                    stack_queries(p, 1)
                    if second:
                        widest_weight(1)
                        widest_weight(2)
                    statistics2(p, 1)
                    sum_squares(p, 1)
                    root_inputs(p, 1)
                    roots(p, 1, 1, 1 if early else 4)
                turn2_lo(p)
                prep_y(p, 0)
                if early:
                    roots(p, 1, 2, 4)
                if second:
                    any_wide_weight()
                roots(p, 1, 5, 7)
                x1_offset(p, 1)
                if first:
                    x_statistics(2, 4, 7)
                if second:
                    prep_y(p, 1)
                qk_upper(p, 1)
                if first:
                    x_statistics(2, 7, 10)
                gate(p, 1, 0)
                qk_double(p, 2)
                up(p, 1, 0)
                gate(p, 1, 1)
                up(p, 1, 1)
                begin(p + 1)

            begin(FIRST)
            run(dve, iteration)
            dve.wait_ge(result_ready, B)
            add_last_pair()

        @block.tensor
        def _(pe):
            pe.wait_ge(ident_ready, 1)
            for m in range(3):
                pe.wait_ge(w_loaded[min(m, 1)], 16 * (1, 2, 2)[m])
                for k in range(KC):
                    for c in range(KC):
                        last = nc.tensor.transpose(w_transposed(m)[:, KC * k + c, :], w_raw[:, m, c, k * P:(k + 1) * P], ident[:])
                last.then_inc(w_turned, 1)

            def claim(p, task):
                k, m = use(p, task)
                if since(m, 2):
                    pe.wait_ge(drained[k], m - 1)
                return k

            def scores(p, e, t):
                b = 2 * p + e
                if not has_tile(p, b):
                    return
                o = OCTETS * b + t
                if t == 0:
                    k, m = use(p, "stackq0") if e else use(p - 1, "stackq1")
                    pe.wait_ge(drained[k], m)
                    if isinstance(b, int) and b == 0:
                        k, m = use(FIRST, "stackk1")
                        pe.wait_ge(drained[k], m)
                    else:
                        pe.wait_ge(km_loaded[e], 64 * (p + e))
                if isinstance(o, int) and o == 0:
                    pe.wait_ge(w_lo_ready, 3)
                if since(o, 2):
                    pe.wait_ge(probs_ready, o - 1)
                for s in range(HEADS_PER_OCTET):
                    h = place(HEADS_PER_OCTET * t + s)[0]
                    last = nc.tensor.matmul(score_ps[t % 2][:, s, :], k_masked[:, e, h % 4, h // 4, :],
                                            q_stack[:, e, h // 4, :], start=True, stop=True)
                last.then_inc(scores_ready, 1)

            def weigh(p, e, t):
                b = 2 * p + e
                o = OCTETS * b + t - 1
                e, t = (e, t - 1) if t else (1 - e, OCTETS - 1)
                b = b if t < OCTETS - 1 else b - 1
                if not has_tile(p, b):
                    return
                pe.wait_ge(probs_ready, o + 1)
                if t == 0:
                    pe.wait_ge(v_ready_of(p, b, e)[0], v_ready_of(p, b, e)[1])
                    if since(b, 1):
                        pe.wait_ge(o_turned_ready, b)
                for s in range(HEADS_PER_OCTET):
                    h, region, quadrant, i = place(HEADS_PER_OCTET * t + s)
                    last = nc.tensor.matmul(pv_ps[BLOCK * quadrant:BLOCK * (quadrant + 1), region * P:(region + 1) * P],
                                            v_blocks[:, e, h * BLOCK:(h + 1) * BLOCK],
                                            probs[:, t % 2, s * P:(s + 1) * P],
                                            start=(i == 0), stop=(i == (2 if region < 2 else 1)),
                                            tile_position=(0, BLOCK * quadrant))
                last.then_inc(pv_done, 1)

            def v_ready_of(p, b, e):
                if e == 0:
                    k, m = use(p - 1, "v1")
                    return drained[k], m
                k, m = use(p, "v0")
                return drained[k], m

            def turn(p, e):
                b = 2 * p + e
                if not has_tile(p, b + 2):
                    return
                k = claim(p, f"turn{e}")
                pe.wait_ge(ctx_loaded[e], 16 * (p + 2))
                for c in range(KC):
                    last = nc.tensor.transpose(bank[k][:, (KC + c) * P:(KC + c + 1) * P], ctx_sb[:, e, c * P:(c + 1) * P], ident[:])
                last.then_inc(ctx_turned, 1)
                pe.wait_ge(xn_ready, b + 3)
                for c in range(KC):
                    last = nc.tensor.transpose(bank[k][:, c * P:(c + 1) * P], xn[:, e, c * P:(c + 1) * P], ident[:])
                last.then_inc(filled[k], 1)

            def project(dst, tile, source, column):
                n = 0
                for c in range(KC):
                    for a, w in ((xc_hi, w_hi), (xc_hi, w_lo), (xc_lo, w_hi)):
                        n += 1
                        last = nc.tensor.matmul(dst, a[:, tile, KC * source + c, :], w[:, c, column * D:(column + 1) * D],
                                                start=(n == 1), stop=(n == 3 * KC))
                return last

            def queries_keys(p, e):
                b = 2 * p + e
                if not has_tile(p, b + 2):
                    return
                k = claim(p, f"qk{e}")
                j, m = use(p, f"turn{e}")
                pe.wait_ge(drained[j], m)
                if isinstance(b, int) and b == -2:
                    pe.wait_ge(w_lo_ready, 2)
                project(bank[k][:, 0:D], e, 0, 0)
                project(bank[k][:, D:2 * D], e, 1, 1).then_inc(filled[k], 1)

            def values(p, e):
                b = 2 * p + e
                if not has_tile(p, b + 1):
                    return
                k = claim(p, f"v{e}")
                if isinstance(b, int) and b == -1:
                    pe.wait_ge(w_lo_ready, 3)
                project(bank[k][:, 0:D], 1 - e, 1, 2).then_inc(filled[k], 1)

            def stacks(p, e):
                b = 2 * p + e
                if not has_tile(p, b + 1):
                    return
                if isinstance(b, int) and b == -1:
                    pe.wait_ge(ident16_ready, 1)
                for name in ("stackq", "stackk"):
                    k = claim(p, f"{name}{e}")
                    if name == "stackq":
                        pe.wait_ge(qk_parts_ready, b + 2)
                    dst = bank[k][:].bitcast(F16)
                    for g in range(GROUPS):
                        h = 4 * g + (0 if name == "stackq" else H)
                        src = qk_parts[:, h:h + 4, :, :].rearrange("p h a d -> p (h a d)")
                        last = nc.tensor.transpose(dst[:, g * P:(g + 1) * P], src, ident16[:])
                    last.then_inc(filled[k], 1)

            def out_rows(p, e):
                b = 2 * p + e
                if not has_tile(p, b - 1):
                    return
                k = claim(p, f"out{e}")
                pe.wait_ge(o_turned_ready, b)
                for r in range(3):
                    last = nc.tensor.transpose(bank[k][:, r * P:(r + 1) * P], o_turned[:, 1 - e, r * P:(r + 1) * P], ident[:])
                last.then_inc(filled[k], 1)

            def prep(task):
                part = PREP[task]
                k = claim(0, task)
                pe.wait_ge(w_converted, 1)
                if part < NJ:
                    r = rows(part)
                    for a in range(2):
                        for c in range(KC):
                            col = (KC * a + c) * P
                            last = nc.tensor.transpose(bank[k][:, col:col + r], gu_raw[0:r, a, part, c * P:(c + 1) * P], ident[0:r, 0:r])
                else:
                    for a in range(2):
                        j = 2 * (part - NJ) + a
                        for c in range(KC):
                            col = a * D + c * P
                            last = nc.tensor.transpose(bank[k][0:rows(j), col:col + P], dn_raw[:, c, j * P:j * P + rows(j)], ident[:])
                last.then_inc(filled[k], 1)

            def turn2(p):
                if not here(p, "turn2"):
                    return
                if isinstance(p, int) and p == 0:
                    return prep("turn2")
                k = claim(p, "turn2")
                pe.wait_ge(x1n_ready, 2 * p)
                for c in range(KC):
                    for e in range(2):
                        last = nc.tensor.transpose(bank[k][:, c * TOK + e * P:c * TOK + (e + 1) * P], x1n[:, e, c * P:(c + 1) * P], ident[:])
                last.then_inc(filled[k], 1)

            def chunk(p, j, wide_weights):
                task = f"ffn{j}"
                if not here(p, task):
                    return
                if isinstance(p, int) and p == 0:
                    return prep(task)
                k = claim(p, task)
                if j == 0:
                    i, m = use(p, "turn2")
                    pe.wait_ge(drained[i], m)
                r = rows(j)
                for a in range(2):
                    n = 0
                    for c in range(KC):
                        for w, xx in products(wide_weights, gu_hi, gu_lo, x2_hi, x2_lo):
                            n += 1
                            last = nc.tensor.matmul(bank[k][0:r, a * TOK:(a + 1) * TOK], w[:, j, a, c, 0:r], xx[:, c, :],
                                                    start=(n == 1), stop=(n == (4 if wide_weights else 2) * KC))
                last.then_inc(filled[k], 1)

            def products(wide_weights, w_upper, w_lower, upper, lower):
                pairs = [(w_upper, upper), (w_upper, lower)]
                return pairs + [(w_lower, upper), (w_lower, lower)] if wide_weights else pairs

            def down(p, e, wide_weights):
                task = f"y{e}"
                if not here(p, task):
                    return
                if isinstance(p, int) and p == 0:
                    return prep(task)
                k = claim(p, task)
                n = 0
                for j in range(NJ):
                    if e == 0:
                        pe.wait_ge(h_lo_ready, NJ * (p - 2) + j + 1)
                    r = rows(j)
                    for w, hh in products(wide_weights, dn_hi, dn_lo, h_hi, h_lo):
                        n += 1
                        last = nc.tensor.matmul(bank[k][:, 0:D], hh[0:r, j, e * P:(e + 1) * P], w[0:r, j, :],
                                                start=(n == 1), stop=(n == (4 if wide_weights else 2) * NJ))
                last.then_inc(filled[k], 1)

            def down_last(wide_weights):
                p = PAIRS + 1
                for chunks in (range(NJ - 2), (NJ - 2,), (NJ - 1,)):
                    for e in range(2):
                        if 0 in chunks:
                            claim(p, f"y{e}")
                        k, _ = use(p, f"y{e}")
                        for j in chunks:
                            if e == 0:
                                pe.wait_ge(h_lo_ready, NJ * (p - 2) + j + 1)
                            r = rows(j)
                            pairs = products(wide_weights, dn_hi, dn_lo, h_hi, h_lo)
                            for n, (w, hh) in enumerate(pairs):
                                last = nc.tensor.matmul(bank[k][:, 0:D], hh[0:r, j, e * P:(e + 1) * P], w[0:r, j, :],
                                                        start=(j == 0 and n == 0), stop=(j == NJ - 1 and n == len(pairs) - 1))
                        if j == NJ - 1:
                            last.then_inc(filled[k], 1)

            def iteration(p, wide_weights=False):
                weigh(p, 0, 0)
                scores(p, 0, 0)
                turn(p, 0)

                scores(p, 0, 1)
                out_rows(p, 0)
                weigh(p, 0, 1)
                values(p, 0)
                stacks(p, 0)
                queries_keys(p, 0)

                scores(p, 0, 2)
                weigh(p, 0, 2)
                chunk(p, 2, wide_weights)
                chunk(p, 3, wide_weights)

                scores(p, 0, 3)
                weigh(p, 0, 3)
                chunk(p, 4, wide_weights)

                weigh(p, 1, 0)
                scores(p, 1, 0)
                chunk(p, 5, wide_weights)
                turn(p, 1)

                scores(p, 1, 1)
                out_rows(p, 1)
                weigh(p, 1, 1)
                values(p, 1)
                if isinstance(p, int) and p == FIRST:
                    queries_keys(p, 1)
                    stacks(p, 1)
                else:
                    stacks(p, 1)
                    queries_keys(p, 1)
                turn2(p)

                scores(p, 1, 2)
                weigh(p, 1, 2)
                if isinstance(p, int) and p == PAIRS + 1:
                    return down_last(wide_weights)
                down(p, 0, wide_weights)

                scores(p, 1, 3)
                weigh(p, 1, 3)
                down(p, 1, wide_weights)
                chunk(p, 0, wide_weights)
                chunk(p, 1, wide_weights)

            for p in range(FIRST, 1):
                iteration(p)
            pe.wait_ge(w_max_steps, 8)
            any_wide = pe.alloc_register("any_wide")
            pe.reg_load(any_wide, wide[:])
            with pe.If_ne(any_wide, 0):
                run(pe, lambda p: iteration(p, True), 1)
            with pe.Else():
                run(pe, lambda p: iteration(p, False), 1)


INPUTS = ["x", "ctx_2048", "g_xattn", "g_ffn", "L0_xattn_Wq", "L0_xattn_Wk", "L0_xattn_Wv", "L0_ffn_wq_gate",
          "L0_ffn_s_gate", "L0_ffn_wq_up", "L0_ffn_s_up", "L0_ffn_wq_down", "L0_ffn_s_down"]


def kernel(**inputs):
    import numpy as np
    import concourse.bacc as bacc
    from concourse.bass_utils import run_bass_kernel_spmd

    nc = bacc.Bacc("TRN2", target_bir_lowering=False, num_devices=1)
    arrays, args = {}, []
    for name in INPUTS:
        a = np.ascontiguousarray(inputs[name])
        arrays[f"{name}_dram"] = a
        args.append(nc.dram_tensor(f"{name}_dram", a.shape, mybir.dt.from_np(a.dtype), kind="ExternalInput").ap())
    x = arrays["x_dram"]
    args.append(nc.dram_tensor("out_dram", x.shape, mybir.dt.from_np(x.dtype), kind="ExternalOutput").ap())
    build_program(nc, *args)
    result = run_bass_kernel_spmd(nc, [arrays], core_ids=[0])
    return result.results[0]["out_dram"]
```
